# Optimizing a Trainium2 kernel written in Bass

```python
import numpy as np
import jax
import jax.numpy as jnp

def _softmax(x, axis=-1):
    return jax.nn.softmax(x, axis=axis)

def _gelu(x):
    return jax.nn.gelu(x, approximate=True)

def _silu(x):
    return jax.nn.silu(x)

def _sigmoid(x):
    return jax.nn.sigmoid(x)

def _layernorm(x, axis=-1, eps=1e-05):
    m = jnp.mean(x, axis=axis, keepdims=True)
    v = jnp.var(x, axis=axis, keepdims=True)
    return (x - m) / jnp.sqrt(v + eps)

def _scatter_add(tgt, idx, src, axis=0):
    return tgt.at[idx].add(src)

def _segment_sum(src, seg, n):
    return jax.ops.segment_sum(src, seg, n)
kernel_name = 'mk_gps_d2_gnn_r8_9a500f'

def setup_inputs(seed: int=0):
    np.random.seed(seed)
    _w = jnp.asarray

    def _rec_inputs():
        import jax
        import jax.numpy as jnp
        _gk = jax.random.key(seed)
        x = -0.0002117 + 1 * jax.random.normal(jax.random.fold_in(_gk, 1), (12500, 256), jnp.float32)
        _s = jax.random.randint(jax.random.fold_in(_gk, 2), (100000,), 0, 12500, jnp.int32)
        _d = jax.random.randint(jax.random.fold_in(_gk, 3), (100000,), 0, 12500, jnp.int32)
        _loop = jnp.arange(12500, dtype=jnp.int32)
        src = jnp.concatenate([_s, _d, _loop])
        dst = jnp.concatenate([_d, _s, _loop])
        _o = jnp.argsort(dst, stable=True)
        src = src[_o]
        dst = dst[_o]
        edge_weight = jax.random.uniform(jax.random.fold_in(_gk, 13), (212500,), jnp.float32, 0.0, 0.999998)
        return (x, src, dst, edge_weight)
    x, src, dst, edge_weight = _rec_inputs()

    def _L0_gnn_setup():
        import jax, jax.numpy as jnp
        import numpy as np
        N_NODES = 12500
        N_EDGES = 37500
        D = 256
        EPS = 1e-05
        ALPHA = 0.5

        def gcn_residual(x, edge_index, edge_weight, W, b, gamma, beta):
            src, dst = (edge_index[0], edge_index[1])
            h = x @ W
            deg = jax.ops.segment_sum(edge_weight, dst, num_segments=N_NODES) + 1.0
            dinv = jax.lax.rsqrt(deg)
            norm = dinv[src] * edge_weight * dinv[dst]
            agg = jax.ops.segment_sum(norm[:, None] * h[src], dst, num_segments=N_NODES)
            agg = agg + (dinv * dinv)[:, None] * h
            h = agg + b
            mu = jnp.mean(h, axis=-1, keepdims=True)
            var = jnp.mean(jnp.square(h - mu), axis=-1, keepdims=True)
            h = (h - mu) * jax.lax.rsqrt(var + EPS) * gamma + beta
            h = ALPHA * h + (1.0 - ALPHA) * x
            return jax.nn.relu(h)
        key = jax.random.key(seed)
        ks = jax.random.split(key, 6)
        x = jax.random.normal(ks[0], (N_NODES, D), dtype=jnp.float32)
        edge_index = jax.random.randint(ks[1], (2, N_EDGES), 0, N_NODES, dtype=jnp.int32)
        edge_weight = jax.random.uniform(ks[2], (N_EDGES,), dtype=jnp.float32)
        W = jax.random.normal(ks[3], (D, D), dtype=jnp.float32) / np.float32(np.sqrt(D))
        b = 0.01 * jax.random.normal(ks[4], (D,), dtype=jnp.float32)
        gamma = jnp.ones((D,), dtype=jnp.float32)
        beta = jnp.zeros((D,), dtype=jnp.float32)
        return {'x': x, 'edge_index': edge_index, 'edge_weight': edge_weight, 'W': W, 'b': b, 'gamma': gamma, 'beta': beta}
    _L0_gnn_all = _L0_gnn_setup()
    _L0_gnn_in = {k: v for k, v in _L0_gnn_all.items() if k in ('W', 'b', 'gamma', 'beta')}
    del _L0_gnn_all

    def _L0_mix_setup():
        import jax, jax.numpy as jnp
        import numpy as np
        HEADS = 8
        DIM_HEAD = 32
        SCALE = DIM_HEAD ** (-0.5)
        EPS = 1e-05

        def _layernorm_gamma(x, gamma):
            mu = jnp.mean(x, axis=-1, keepdims=True)
            var = jnp.var(x, axis=-1, keepdims=True)
            return (x - mu) * jax.lax.rsqrt(var + EPS) * gamma
        key = jax.random.key(seed)
        k1, k2, k3 = jax.random.split(key, 3)
        B, N, D = (8, 2048, 256)
        hidden = HEADS * DIM_HEAD
        x = jax.random.normal(k1, (B, N, D), dtype=jnp.float32)
        Wqkv = jax.random.normal(k2, (D, 3 * hidden), dtype=jnp.float32) * D ** (-0.5)
        Wout = jax.random.normal(k3, (hidden, D), dtype=jnp.float32) * hidden ** (-0.5)
        gamma = jnp.ones((D,), dtype=jnp.float32)
        return {'x': x, 'Wqkv': Wqkv, 'Wout': Wout, 'gamma': gamma}
    _L0_mix_all = _L0_mix_setup()
    _L0_mix_in = {k: v for k, v in _L0_mix_all.items() if k in ('Wqkv', 'Wout', 'gamma')}
    del _L0_mix_all

    def _L0_ffn_setup():
        import jax, jax.numpy as jnp
        import numpy as np
        NUM_EXPERTS = 8
        TOP_K = 2
        B, S, D = (8, 1024, 256)

        def _moe(tokens, router_w, w1, b1, w2, b2):
            N = tokens.shape[0]
            E = router_w.shape[0]
            logits = tokens.astype(jnp.float32) @ router_w.astype(jnp.float32).T
            probs = jax.nn.softmax(logits, axis=-1)
            rw, re = jax.lax.top_k(probs, TOP_K)
            if TOP_K > 1:
                rw = rw / jnp.maximum(rw.sum(-1, keepdims=True), 1e-12)
            rw = rw.astype(tokens.dtype)
            combine = jnp.zeros((N, E), tokens.dtype).at[jnp.arange(N)[:, None], re].set(rw)
            out = tokens
            for e in range(E):
                h = jax.nn.gelu(tokens @ w1[e] + b1[e], approximate=False)
                y = h @ w2[e] + b2[e]
                out = out + combine[:, e:e + 1] * y
            return out
        key = jax.random.key(seed)
        ks = jax.random.split(key, 4)
        scale = 1.0 / np.sqrt(D).astype(np.float32)
        return {'input_embeddings': jax.random.normal(ks[0], (B, S, D), jnp.float32), 'router_w': jax.random.normal(ks[1], (NUM_EXPERTS, D), jnp.float32) * scale, 'w1': jax.random.normal(ks[2], (NUM_EXPERTS, D, D), jnp.float32) * scale, 'b1': jnp.zeros((NUM_EXPERTS, D), jnp.float32), 'w2': jax.random.normal(ks[3], (NUM_EXPERTS, D, D), jnp.float32) * scale, 'b2': jnp.zeros((NUM_EXPERTS, D), jnp.float32)}
    _L0_ffn_all = _L0_ffn_setup()
    _L0_ffn_in = {k: v for k, v in _L0_ffn_all.items() if k in ('router_w', 'w1', 'b1', 'w2', 'b2')}
    del _L0_ffn_all

    def _L1_gnn_setup():
        import jax, jax.numpy as jnp
        import numpy as np
        N_NODES = 12500
        N_EDGES = 400000
        IN_FT = 256
        OUT_FT = 256
        key = jax.random.key(seed)
        k1, k2, k3, k4, k5 = jax.random.split(key, 5)
        seq = jax.random.normal(k1, (N_NODES, IN_FT), dtype=jnp.float32)
        edge_row = jax.random.randint(k2, (N_EDGES,), 0, N_NODES, dtype=jnp.int32)
        edge_col = jax.random.randint(k3, (N_EDGES,), 0, N_NODES, dtype=jnp.int32)
        edge_vals = jax.random.uniform(k4, (N_EDGES,), dtype=jnp.float32)
        std = 1.414 * np.sqrt(2.0 / (IN_FT + OUT_FT))
        W = jax.random.normal(k5, (OUT_FT, IN_FT), dtype=jnp.float32) * std
        bias = jnp.zeros((OUT_FT,), dtype=jnp.float32)
        return {'seq': seq, 'edge_row': edge_row, 'edge_col': edge_col, 'edge_vals': edge_vals, 'W': W, 'bias': bias}
    _L1_gnn_all = _L1_gnn_setup()
    _L1_gnn_in = {k: v for k, v in _L1_gnn_all.items() if k in ('W', 'bias')}
    del _L1_gnn_all

    def _L1_mix_setup():
        import jax, jax.numpy as jnp
        import numpy as np
        D_MODEL = 256
        NHEAD = 8
        D_HEAD = D_MODEL // NHEAD
        DIM_FF = 1024
        B, L = (4, 2048)
        LN_EPS = 1e-05

        def _layernorm(x, g, b):
            mu = jnp.mean(x, axis=-1, keepdims=True)
            var = jnp.mean((x - mu) ** 2, axis=-1, keepdims=True)
            return (x - mu) * jax.lax.rsqrt(var + LN_EPS) * g + b

        def _phi(x):
            return jnp.where(x > 0, x + 1.0, jnp.exp(x))
        key = jax.random.key(seed)
        ks = jax.random.split(key, 16)
        s_in = 1.0 / np.sqrt(D_MODEL)
        s_ff = 1.0 / np.sqrt(DIM_FF)
        inp = {'x': jax.random.normal(ks[0], (B, L, D_MODEL), dtype=jnp.float32), 'Wq': jax.random.normal(ks[1], (D_MODEL, D_MODEL), dtype=jnp.float32) * s_in, 'bq': jnp.zeros((D_MODEL,), jnp.float32), 'Wk': jax.random.normal(ks[2], (D_MODEL, D_MODEL), dtype=jnp.float32) * s_in, 'bk': jnp.zeros((D_MODEL,), jnp.float32), 'Wv': jax.random.normal(ks[3], (D_MODEL, D_MODEL), dtype=jnp.float32) * s_in, 'bv': jnp.zeros((D_MODEL,), jnp.float32), 'Wo': jax.random.normal(ks[4], (D_MODEL, D_MODEL), dtype=jnp.float32) * s_in, 'bo': jnp.zeros((D_MODEL,), jnp.float32), 'W1': jax.random.normal(ks[5], (D_MODEL, DIM_FF), dtype=jnp.float32) * s_in, 'b1': jnp.zeros((DIM_FF,), jnp.float32), 'W2': jax.random.normal(ks[6], (DIM_FF, D_MODEL), dtype=jnp.float32) * s_ff, 'b2': jnp.zeros((D_MODEL,), jnp.float32), 'ln1_g': jnp.ones((D_MODEL,), jnp.float32), 'ln1_b': jnp.zeros((D_MODEL,), jnp.float32), 'ln2_g': jnp.ones((D_MODEL,), jnp.float32), 'ln2_b': jnp.zeros((D_MODEL,), jnp.float32)}
        return inp
    _L1_mix_all = _L1_mix_setup()
    _L1_mix_in = {k: v for k, v in _L1_mix_all.items() if k in ('Wq', 'bq', 'Wk', 'bk', 'Wv', 'bv', 'Wo', 'bo', 'W1', 'b1', 'W2', 'b2', 'ln1_g', 'ln1_b', 'ln2_g', 'ln2_b')}
    del _L1_mix_all

    def _L1_ffn_setup():
        import jax, jax.numpy as jnp
        import numpy as np
        DIM = 256
        H = 8
        D = 64
        G = 64
        INNER = H * D
        SCALE = D ** (-0.5)
        key = jax.random.key(seed)
        ks = jax.random.split(key, 12)
        B, N = (4, 2048)
        x = jax.random.normal(ks[0], (B, N, DIM), dtype=jnp.float32)
        s = lambda fan_in: 1.0 / np.sqrt(fan_in)
        W_fx = jax.random.normal(ks[1], (DIM, INNER), dtype=jnp.float32) * s(DIM)
        b_fx = jnp.zeros((INNER,), dtype=jnp.float32)
        W_x = jax.random.normal(ks[2], (DIM, INNER), dtype=jnp.float32) * s(DIM)
        b_x = jnp.zeros((INNER,), dtype=jnp.float32)
        A = jax.random.normal(ks[3], (G, D), dtype=jnp.float32)
        Q, _ = jnp.linalg.qr(A.T)
        W_slice = Q[:, :G].astype(jnp.float32)
        b_slice = jnp.zeros((G,), dtype=jnp.float32)
        W_q = jax.random.normal(ks[4], (D, D), dtype=jnp.float32) * s(D)
        W_k = jax.random.normal(ks[5], (D, D), dtype=jnp.float32) * s(D)
        W_v = jax.random.normal(ks[6], (D, D), dtype=jnp.float32) * s(D)
        W_out = jax.random.normal(ks[7], (INNER, DIM), dtype=jnp.float32) * s(INNER)
        b_out = jnp.zeros((DIM,), dtype=jnp.float32)
        temperature = jnp.ones((1, H, 1, 1), dtype=jnp.float32) * 0.5
        return {'x': x, 'W_fx': W_fx, 'b_fx': b_fx, 'W_x': W_x, 'b_x': b_x, 'W_slice': W_slice, 'b_slice': b_slice, 'W_q': W_q, 'W_k': W_k, 'W_v': W_v, 'W_out': W_out, 'b_out': b_out, 'temperature': temperature}
    _L1_ffn_all = _L1_ffn_setup()
    _L1_ffn_in = {k: v for k, v in _L1_ffn_all.items() if k in ('W_fx', 'b_fx', 'W_x', 'b_x', 'W_slice', 'b_slice', 'W_q', 'W_k', 'W_v', 'W_out', 'b_out', 'temperature')}
    del _L1_ffn_all
    return {'x': x, 'src': src, 'dst': dst, 'edge_weight': edge_weight, 'L0_gnn_W': _L0_gnn_in['W'], 'L0_gnn_b': _L0_gnn_in['b'], 'L0_gnn_gamma': _L0_gnn_in['gamma'], 'L0_gnn_beta': _L0_gnn_in['beta'], 'L0_mix_Wqkv': _L0_mix_in['Wqkv'], 'L0_mix_Wout': _L0_mix_in['Wout'], 'L0_mix_gamma': _L0_mix_in['gamma'], 'L0_ffn_router_w': _L0_ffn_in['router_w'], 'L0_ffn_w1': _L0_ffn_in['w1'], 'L0_ffn_b1': _L0_ffn_in['b1'], 'L0_ffn_w2': _L0_ffn_in['w2'], 'L0_ffn_b2': _L0_ffn_in['b2'], 'L1_gnn_W': _L1_gnn_in['W'], 'L1_gnn_bias': _L1_gnn_in['bias'], 'L1_mix_Wq': _L1_mix_in['Wq'], 'L1_mix_bq': _L1_mix_in['bq'], 'L1_mix_Wk': _L1_mix_in['Wk'], 'L1_mix_bk': _L1_mix_in['bk'], 'L1_mix_Wv': _L1_mix_in['Wv'], 'L1_mix_bv': _L1_mix_in['bv'], 'L1_mix_Wo': _L1_mix_in['Wo'], 'L1_mix_bo': _L1_mix_in['bo'], 'L1_mix_W1': _L1_mix_in['W1'], 'L1_mix_b1': _L1_mix_in['b1'], 'L1_mix_W2': _L1_mix_in['W2'], 'L1_mix_b2': _L1_mix_in['b2'], 'L1_mix_ln1_g': _L1_mix_in['ln1_g'], 'L1_mix_ln1_b': _L1_mix_in['ln1_b'], 'L1_mix_ln2_g': _L1_mix_in['ln2_g'], 'L1_mix_ln2_b': _L1_mix_in['ln2_b'], 'L1_ffn_W_fx': _L1_ffn_in['W_fx'], 'L1_ffn_b_fx': _L1_ffn_in['b_fx'], 'L1_ffn_W_x': _L1_ffn_in['W_x'], 'L1_ffn_b_x': _L1_ffn_in['b_x'], 'L1_ffn_W_slice': _L1_ffn_in['W_slice'], 'L1_ffn_b_slice': _L1_ffn_in['b_slice'], 'L1_ffn_W_q': _L1_ffn_in['W_q'], 'L1_ffn_W_k': _L1_ffn_in['W_k'], 'L1_ffn_W_v': _L1_ffn_in['W_v'], 'L1_ffn_W_out': _L1_ffn_in['W_out'], 'L1_ffn_b_out': _L1_ffn_in['b_out'], 'L1_ffn_temperature': _L1_ffn_in['temperature']}

def reference(x, src, dst, edge_weight, L0_gnn_W, L0_gnn_b, L0_gnn_gamma, L0_gnn_beta, L0_mix_Wqkv, L0_mix_Wout, L0_mix_gamma, L0_ffn_router_w, L0_ffn_w1, L0_ffn_b1, L0_ffn_w2, L0_ffn_b2, L1_gnn_W, L1_gnn_bias, L1_mix_Wq, L1_mix_bq, L1_mix_Wk, L1_mix_bk, L1_mix_Wv, L1_mix_bv, L1_mix_Wo, L1_mix_bo, L1_mix_W1, L1_mix_b1, L1_mix_W2, L1_mix_b2, L1_mix_ln1_g, L1_mix_ln1_b, L1_mix_ln2_g, L1_mix_ln2_b, L1_ffn_W_fx, L1_ffn_b_fx, L1_ffn_W_x, L1_ffn_b_x, L1_ffn_W_slice, L1_ffn_b_slice, L1_ffn_W_q, L1_ffn_W_k, L1_ffn_W_v, L1_ffn_W_out, L1_ffn_b_out, L1_ffn_temperature):
    import jax
    import jax.numpy as jnp

    def _L0_gnn_ref(x, edge_index, edge_weight, W, b, gamma, beta):
        import jax, jax.numpy as jnp
        import numpy as np
        N_NODES = 12500
        N_EDGES = 37500
        D = 256
        EPS = 1e-05
        ALPHA = 0.5

        def gcn_residual(x, edge_index, edge_weight, W, b, gamma, beta):
            src, dst = (edge_index[0], edge_index[1])
            h = x @ W
            deg = jax.ops.segment_sum(edge_weight, dst, num_segments=N_NODES) + 1.0
            dinv = jax.lax.rsqrt(deg)
            norm = dinv[src] * edge_weight * dinv[dst]
            agg = jax.ops.segment_sum(norm[:, None] * h[src], dst, num_segments=N_NODES)
            agg = agg + (dinv * dinv)[:, None] * h
            h = agg + b
            mu = jnp.mean(h, axis=-1, keepdims=True)
            var = jnp.mean(jnp.square(h - mu), axis=-1, keepdims=True)
            h = (h - mu) * jax.lax.rsqrt(var + EPS) * gamma + beta
            h = ALPHA * h + (1.0 - ALPHA) * x
            return jax.nn.relu(h)
        return gcn_residual(x, edge_index, edge_weight, W, b, gamma, beta)

    def _L0_mix_ref(x, Wqkv, Wout, gamma):
        import jax, jax.numpy as jnp
        import numpy as np
        HEADS = 8
        DIM_HEAD = 32
        SCALE = DIM_HEAD ** (-0.5)
        EPS = 1e-05

        def _layernorm_gamma(x, gamma):
            mu = jnp.mean(x, axis=-1, keepdims=True)
            var = jnp.var(x, axis=-1, keepdims=True)
            return (x - mu) * jax.lax.rsqrt(var + EPS) * gamma
        B, N, D = x.shape
        qkv = x @ Wqkv
        q, k, v = jnp.split(qkv, 3, axis=-1)

        def to_heads(t):
            return t.reshape(B, N, HEADS, DIM_HEAD).transpose(0, 2, 1, 3)
        q, k, v = map(to_heads, (q, k, v))
        q = jax.nn.softmax(q, axis=-1) * SCALE
        k = jax.nn.softmax(k, axis=2)
        context = jnp.einsum('bhnd,bhne->bhde', k, v)
        out = jnp.einsum('bhde,bhnd->bhne', context, q)
        out = out.transpose(0, 2, 1, 3).reshape(B, N, HEADS * DIM_HEAD)
        out = out @ Wout
        return _layernorm_gamma(out, gamma)

    def _L0_ffn_ref(input_embeddings, router_w, w1, b1, w2, b2):
        import jax, jax.numpy as jnp
        import numpy as np
        NUM_EXPERTS = 8
        TOP_K = 2
        B, S, D = (8, 1024, 256)

        def _moe(tokens, router_w, w1, b1, w2, b2):
            N = tokens.shape[0]
            E = router_w.shape[0]
            logits = tokens.astype(jnp.float32) @ router_w.astype(jnp.float32).T
            probs = jax.nn.softmax(logits, axis=-1)
            rw, re = jax.lax.top_k(probs, TOP_K)
            if TOP_K > 1:
                rw = rw / jnp.maximum(rw.sum(-1, keepdims=True), 1e-12)
            rw = rw.astype(tokens.dtype)
            combine = jnp.zeros((N, E), tokens.dtype).at[jnp.arange(N)[:, None], re].set(rw)
            out = tokens
            for e in range(E):
                h = jax.nn.gelu(tokens @ w1[e] + b1[e], approximate=False)
                y = h @ w2[e] + b2[e]
                out = out + combine[:, e:e + 1] * y
            return out
        b, s, d = input_embeddings.shape
        tokens = input_embeddings.reshape(b * s, d)
        return _moe(tokens, router_w, w1, b1, w2, b2).reshape(b, s, d)

    def _L1_gnn_ref(seq, edge_row, edge_col, edge_vals, W, bias):
        import jax, jax.numpy as jnp
        import numpy as np
        N_NODES = 12500
        N_EDGES = 400000
        IN_FT = 256
        OUT_FT = 256
        seq_fts = jnp.einsum('ni,oi->no', seq, W)
        messages = edge_vals[:, None] * seq_fts[edge_col]
        out = jax.ops.segment_sum(messages, edge_row, num_segments=N_NODES)
        return jax.nn.relu(out + bias)

    def _L1_mix_ref(x, Wq, bq, Wk, bk, Wv, bv, Wo, bo, W1, b1, W2, b2, ln1_g, ln1_b, ln2_g, ln2_b):
        import jax, jax.numpy as jnp
        import numpy as np
        D_MODEL = 256
        NHEAD = 8
        D_HEAD = D_MODEL // NHEAD
        DIM_FF = 1024
        B, L = (4, 2048)
        LN_EPS = 1e-05

        def _layernorm(x, g, b):
            mu = jnp.mean(x, axis=-1, keepdims=True)
            var = jnp.mean((x - mu) ** 2, axis=-1, keepdims=True)
            return (x - mu) * jax.lax.rsqrt(var + LN_EPS) * g + b

        def _phi(x):
            return jnp.where(x > 0, x + 1.0, jnp.exp(x))
        Bq, Lq, _ = x.shape
        q = (x @ Wq + bq).reshape(Bq, Lq, NHEAD, D_HEAD)
        k = (x @ Wk + bk).reshape(Bq, Lq, NHEAD, D_HEAD)
        v = (x @ Wv + bv).reshape(Bq, Lq, NHEAD, D_HEAD)
        q_phi = _phi(q)
        k_phi = _phi(k)
        kv = jnp.einsum('blhd,blhe->bhde', k_phi, v)
        k_sum = k_phi.sum(axis=1)
        z = 1.0 / (jnp.einsum('blhd,bhd->blh', q_phi, k_sum) + 1e-06)
        out = jnp.einsum('blhd,bhde,blh->blhe', q_phi, kv, z)
        out = out.reshape(Bq, Lq, D_MODEL) @ Wo + bo
        x = _layernorm(x + out, ln1_g, ln1_b)
        ff = jax.nn.relu(x @ W1 + b1) @ W2 + b2
        x = _layernorm(x + ff, ln2_g, ln2_b)
        return x

    def _L1_ffn_ref(x, W_fx, b_fx, W_x, b_x, W_slice, b_slice, W_q, W_k, W_v, W_out, b_out, temperature):
        import jax, jax.numpy as jnp
        import numpy as np
        DIM = 256
        H = 8
        D = 64
        G = 64
        INNER = H * D
        SCALE = D ** (-0.5)
        B, N, _ = x.shape
        fx_mid = (x @ W_fx + b_fx).reshape(B, N, H, D).transpose(0, 2, 1, 3)
        x_mid = (x @ W_x + b_x).reshape(B, N, H, D).transpose(0, 2, 1, 3)
        temp = jnp.clip(temperature, 0.1, 5.0)
        slice_weights = jax.nn.softmax((x_mid @ W_slice + b_slice) / temp, axis=-1)
        slice_norm = slice_weights.sum(axis=2)
        slice_token = jnp.einsum('bhnc,bhng->bhgc', fx_mid, slice_weights)
        slice_token = slice_token / (slice_norm[..., None] + 1e-05)
        q = slice_token @ W_q
        k = slice_token @ W_k
        v = slice_token @ W_v
        attn = jax.nn.softmax(jnp.einsum('bhgc,bhkc->bhgk', q, k) * SCALE, axis=-1)
        out_slice = jnp.einsum('bhgk,bhkc->bhgc', attn, v)
        out_x = jnp.einsum('bhgc,bhng->bhnc', out_slice, slice_weights)
        out_x = out_x.transpose(0, 2, 1, 3).reshape(B, N, INNER)
        return out_x @ W_out + b_out
    edge_index = jnp.stack([src, dst])
    xn = _layernorm(x, axis=-1)
    x = x + _L0_gnn_ref(xn, edge_index, edge_weight, L0_gnn_W, L0_gnn_b, L0_gnn_gamma, L0_gnn_beta) + _L0_mix_ref(xn[None], L0_mix_Wqkv, L0_mix_Wout, L0_mix_gamma)[0]
    x = x + _L0_ffn_ref(_layernorm(x, axis=-1)[None], L0_ffn_router_w, L0_ffn_w1, L0_ffn_b1, L0_ffn_w2, L0_ffn_b2)[0]
    xn = _layernorm(x, axis=-1)
    x = x + _L1_gnn_ref(xn, src, dst, edge_weight, L1_gnn_W, L1_gnn_bias) + _L1_mix_ref(xn[None], L1_mix_Wq, L1_mix_bq, L1_mix_Wk, L1_mix_bk, L1_mix_Wv, L1_mix_bv, L1_mix_Wo, L1_mix_bo, L1_mix_W1, L1_mix_b1, L1_mix_W2, L1_mix_b2, L1_mix_ln1_g, L1_mix_ln1_b, L1_mix_ln2_g, L1_mix_ln2_b)[0]
    x = x + _L1_ffn_ref(_layernorm(x, axis=-1)[None], L1_ffn_W_fx, L1_ffn_b_fx, L1_ffn_W_x, L1_ffn_b_x, L1_ffn_W_slice, L1_ffn_b_slice, L1_ffn_W_q, L1_ffn_W_k, L1_ffn_W_v, L1_ffn_W_out, L1_ffn_b_out, L1_ffn_temperature)[0]
    return x

_drawn_inputs = setup_inputs


def setup_inputs(seed=0):
    import zlib

    import numpy as np

    out = dict(_drawn_inputs(seed))
    spreads = {'L0_gnn_gamma': (1.0, 0.2),
     'L0_gnn_beta': (0.0, 0.1),
     'L0_mix_gamma': (1.0, 0.2),
     'L0_ffn_b1': (0.0, 0.373),
     'L0_ffn_b2': (0.0, 0.1),
     'L1_gnn_bias': (0.0, 0.584),
     'L1_mix_bq': (0.0, 2.0),
     'L1_mix_bk': (0.0, 2.0),
     'L1_mix_bv': (0.0, 0.416),
     'L1_mix_bo': (0.0, 0.448),
     'L1_mix_b1': (0.0, 0.715),
     'L1_mix_b2': (0.0, 0.491),
     'L1_mix_ln1_g': (1.0, 0.2),
     'L1_mix_ln1_b': (0.0, 0.38),
     'L1_mix_ln2_g': (1.0, 0.2),
     'L1_mix_ln2_b': (0.0, 0.442),
     'L1_ffn_b_fx': (0.0, 0.423),
     'L1_ffn_b_x': (0.0, 0.8),
     'L1_ffn_b_slice': (0.0, 0.8),
     'L1_ffn_b_out': (0.0, 0.438),
     'L1_ffn_temperature': (0.5, 0.6)}
    factors = {'L0_gnn_b': 3.595,
     'L1_mix_Wq': 8.0,
     'L1_mix_Wk': 70.843,
     'L1_ffn_W_x': 8.0,
     'L1_ffn_W_slice': 8.0,
     'L1_ffn_W_q': 8.0,
     'L1_ffn_W_k': 8.0}
    for name, (base, spread) in spreads.items():
        noise = np.random.default_rng([zlib.crc32(name.encode()), seed]).standard_normal(out[name].shape)
        drawn = base * np.exp(spread * noise) if base else spread * noise
        out[name] = jnp.asarray(drawn.astype(out[name].dtype))
    for name, factor in factors.items():
        out[name] = (out[name] * factor).astype(out[name].dtype)
    return out
```

```python
import concourse.bass as bass
from concourse import mybir
from contextlib import ExitStack

F32 = mybir.dt.float32
I32 = mybir.dt.int32
U32 = mybir.dt.uint32
BF16 = mybir.dt.bfloat16
ALU = mybir.AluOpType
ACT = mybir.ActivationFunctionType
AX = mybir.AxisListType

P = 125
TS = 4
D = 256
H2 = 128
STEPS = 72
GRP = 6
GRPS = STEPS // GRP
SG = 120
LN_EPS = 1e-5


class Shared:
    pass


def allocators(nc, ctx, stage):
    def sb(name, shape, dt=F32):
        return ctx.enter_context(nc.sbuf_tensor(f"{stage}_{name}", shape, dt))

    def pb(name, shape, dt=F32):
        return ctx.enter_context(nc.psum_tensor(f"{stage}_{name}", shape, dt))

    used = []

    def sem(name):
        used.append(nc.alloc_semaphore(f"{stage}_{name}"))
        return used[-1]

    def give_back():
        if used:
            nc.clear_and_free_semaphores(used)
            nc.all_engine_barrier()

    ctx.callback(give_back)
    return sb, pb, sem


def records(nc, k):
    CR, NT, ROWS = k.CR, k.NT, k.ROWS
    with ExitStack() as ctx:
        sb, pb, sem = allocators(nc, ctx, "rec")
        raw = [sb("raw_dst", [NT, CR, P], I32), sb("raw_src", [NT, CR, P], I32), sb("raw_w", [NT, CR, P])]
        flt = [sb("flt_dst", [NT, CR, P]), sb("flt_src", [NT, CR, P])]
        space = k.sums[:, :, :].rearrange("p t d -> p (t d)")
        rec = space[:, 0:3 * ROWS].bitcast(I32).rearrange("p (r f) -> p r f", f=3)
        src_e, quot, quot_f, rest, tile_f = (space[:, n * ROWS:(n + 1) * ROWS] for n in range(3, 8))
        quot_i = quot_f.bitcast(I32)
        ps = [pb(f"ps_rec{n}", [P, 4, 128]) for n in range(4)]
        ins_ = [sem(f"rec_in{n}") for n in range(3)]
        ready = sem("rec_flt")
        turned = sem("rec_turned")
        kept = sem("rec_kept")
        src_kept = sem("rec_src")
        chain = sem("rec_chain")
        src_filed = sem("src_filed")
        stored = sem("stored")
        consts = sem("rec_consts")
        batches = [(f, c, min(4, CR - c)) for f in (1, 0, 2) for c in range(0, CR, 4)]
        per = len(batches) // 3
        block = ctx.enter_context(nc.Block())

        @block.sync
        def _(eng):
            for n, ap in enumerate((k.dst, k.src, k.edge_weight)):
                eng.dma_start(raw[n][:, :, :], ap.rearrange("(p c e) -> p c e", c=CR, e=P)).then_inc(ins_[n], 16)

        @block.gpsimd
        def _(eng):
            eng.iota(k.lane[:], [[1, 128]], base=0, channel_multiplier=0,
                     allow_small_or_imprecise_dtypes=True)
            eng.memset(k.ident[:], 0.0).then_inc(consts, 1)
            eng.wait_ge(consts, 1)
            eng.affine_select(out=k.ident[:], in_=k.ident[:], compare_op=ALU.not_equal, fill=1.0,
                              base=0, pattern=[[-1, 128]], channel_multiplier=1).then_inc(consts, 1)

        @block.scalar
        def _(eng):
            eng.wait_ge(ins_[1], 16)
            eng.copy(flt[1][:, :, :], raw[1][:, :, :]).then_inc(ready, 1)
            eng.wait_ge(ins_[0], 16)
            eng.copy(flt[0][:, :, :], raw[0][:, :, :]).then_inc(ready, 1)
            for n, (f, c, m) in enumerate(batches):
                if f == 1:
                    continue
                eng.wait_ge(turned, n + 1)
                out = rec[:, :, f] if f == 0 else rec[:, :, f].bitcast(F32)
                eng.copy(out.rearrange("e (p c) -> e c p", c=CR)[:, c:c + m, :], ps[n % 4][:, 0:m, 0:NT])\
                   .then_inc(kept, 1)
            eng.wait_ge(kept, 2 * per)
            eng.wait_ge(src_filed, 1)
            eng.dma_start(k.rec_d, rec[:, :, :]).then_inc(stored, 16)
            eng.wait_ge(stored, 16)

        @block.tensor
        def _(eng):
            eng.wait_ge(consts, 2)
            for n, (f, c, m) in enumerate(batches):
                if n % per == 0:
                    if f == 2:
                        eng.wait_ge(ins_[2], 16)
                    else:
                        eng.wait_ge(ready, n // per + 1)
                tile = raw[2] if f == 2 else flt[f]
                if 4 <= n < per + 4:
                    eng.wait_ge(src_kept, n - 3)
                elif n >= per + 4:
                    eng.wait_ge(kept, n - 3 - per)
                for j in range(m):
                    mm = eng.transpose(ps[n % 4][:, j, 0:NT], tile[:, c + j, :], k.ident[0:NT, 0:NT])
                mm.then_inc(turned, 1)

        @block.vector
        def _(eng):
            for n, (f, c, m) in enumerate(batches[:per]):
                eng.wait_ge(turned, n + 1)
                eng.tensor_copy(src_e[:].rearrange("e (p c) -> e c p", c=CR)[:, c:c + m, :], ps[n % 4][:, 0:m, 0:NT])\
                   .then_inc(src_kept, 1)
            eng.wait_ge(src_kept, per)
            done = [0]

            def link(ins):
                done[0] += 1
                ins.then_inc(chain, 1)
                eng.wait_ge(chain, done[0])

            def divide(num, by, out):
                link(eng.tensor_scalar(quot_i[:], num, 1.0 / by, None, ALU.mult))
                link(eng.tensor_copy(quot[:], quot_i[:]))
                link(eng.scalar_tensor_tensor(out=rest[:], in0=quot[:], scalar=-float(by), in1=num,
                                              op0=ALU.mult, op1=ALU.add))
                link(eng.scalar_tensor_tensor(out=quot[:], in0=rest[:], scalar=float(by), in1=quot[:],
                                              op0=ALU.is_ge, op1=ALU.add))
                link(eng.tensor_scalar(rest[:], rest[:], 0.0, None, ALU.is_lt))
                link(eng.tensor_tensor(out, quot[:], rest[:], ALU.subtract))

            eng.tensor_copy(rec[:, :, 1], src_e[:]).then_inc(src_filed, 1)
            link(eng.memset(k.src_tile[:, ROWS:], 0.0))
            divide(src_e[:], P, tile_f[:])
            link(eng.tensor_copy(k.src_tile[:, 0:ROWS], tile_f[:]))
            divide(tile_f[:], 10, src_e[:])
            link(eng.tensor_copy(k.digit_hi[:], src_e[:]))
            link(eng.scalar_tensor_tensor(out=k.digit_lo[:], in0=src_e[:], scalar=-10.0, in1=tile_f[:],
                                          op0=ALU.mult, op1=ALU.add))


def plan(nc, k, layer):
    NT, ROWS, NS = k.NT, k.ROWS, k.NS
    NG = NS // SG
    CR = ROWS // NT
    NB = NT + 1
    with ExitStack() as ctx:
        sb, pb, sem = allocators(nc, ctx, f"plan{layer}")
        dst_all = sb("dst_all", [NT, CR, P], I32)
        row_last = sb("row_last", [NT, CR])
        bound_row = sb("bound_row", [NT, NB])
        bound_col = sb("bound_col", [NB, 1])
        less = sb("less", [NT, NB])
        ones = sb("plan_ones", [128, 1])
        before = sb("before", [NB, 1])
        before_i = sb("before_i", [NB, 1], I32)
        cut_i = sb("cut_i", [NB, P], I32)
        cut = sb("cut", [NB, P])
        cut_lt = sb("cut_lt", [NB, P])
        inside = sb("inside", [NB, 1])
        first = sb("first", [NB, 1])
        last = sb("last", [NB, 1])
        nfirst = sb("nfirst", [NB, 1])
        diff = sb("diff", [NB, NB])
        tri_ge = sb("tri_ge", [NB, NB])
        tri_gt = sb("tri_gt", [NB, NB])
        start = sb("start", [NB, 1])
        jump = sb("jump", [NB, 2])
        step_row = sb("step_row", [NB, NS])
        reached = sb("reached", [NB, NS])
        step_of = sb("step_of", [SG, NG])
        row_f = sb("row_f", [SG, NG])
        row_i = sb("row_i", [SG, NG], I32)
        ntile_col = sb("ntile_col", [SG, NG])
        if layer == 0:
            src_g = sb("src_g", [SG, NG, P], I32)[:, :, :]
            dst_g = sb("dst_g", [SG, NG, P], I32)[:, :, :]
            w_g = sb("w_g", [SG, NG, P])[:, :, :]
            fetches = [(src_g, k.src_rows), (dst_g, k.dst_rows), (w_g, k.w_rows)]
        else:
            rec_g = sb("rec_g", [SG, NG, 3 * P], I32)
            fields = rec_g[:, :, :].rearrange("s g (e f) -> s g e f", f=3)
            src_g, dst_g, w_g = fields[:, :, :, 0], fields[:, :, :, 1], fields[:, :, :, 2].bitcast(F32)
            fetches = [(rec_g[:, :, :], k.sorted_rows)]
        src_f = sb("src_f", [SG, 2, P])
        dst_f = sb("dst_f", [SG, 2, P])
        w_f = sb("w_f", [SG, 2, P])
        ps_small = pb("ps_small", [128, 512])
        ps_row = pb("ps_row", [128, 4, 512])
        ps_t = pb("ps_t", [128, 3, 512])

        dst_in = sem("dst_in")
        const_done = sem("const_done")
        ones_done = sem("ones_done")
        vec = sem("plan_vec")
        less_ready = sem("less_ready")
        before_mm = sem("before_mm")
        before_ready = sem("before_ready")
        cut_in = sem("cut_in")
        ends_ready = sem("ends_ready")
        start_mm = sem("start_mm")
        reached_ready = sem("reached_ready")
        steps_mm = sem("steps_mm")
        rows_mm = sem("rows_mm")
        rows_ready = sem("rows_ready")
        edges_in = [sem(f"edges_in{g}") for g in range(NG)]
        edges_f = sem("edges_f")
        turned = sem("turned")
        laid = sem("laid")
        RC = 450 if NS % 450 == 0 else 360
        block = ctx.enter_context(nc.Block())

        @block.sync
        def _(eng):
            if layer == 0:
                eng.dma_start(dst_all[:], k.dst.rearrange("(p c e) -> p c e", c=CR, e=P)).then_inc(dst_in, 16)

        @block.gpsimd
        def _(eng):
            eng.iota(bound_row[:], [[P, NB]], base=0, channel_multiplier=0,
                     allow_small_or_imprecise_dtypes=True).then_inc(const_done, 1)
            eng.iota(bound_col[:], [[0, 1]], base=0, channel_multiplier=P,
                     allow_small_or_imprecise_dtypes=True).then_inc(const_done, 1)
            eng.iota(diff[:], [[1, NB]], base=0, channel_multiplier=-1,
                     allow_small_or_imprecise_dtypes=True).then_inc(const_done, 1)
            eng.iota(step_row[:], [[1, NS]], base=0, channel_multiplier=0,
                     allow_small_or_imprecise_dtypes=True).then_inc(const_done, 1)
            eng.iota(step_of[:], [[SG, NG]], base=0, channel_multiplier=1,
                     allow_small_or_imprecise_dtypes=True).then_inc(const_done, 1)
            if layer == 0:
                eng.wait_ge(before_ready, 1)
                eng.nop(nofuse=True)
                eng.indirect_dma_start(out=cut_i[:], out_offset=None, in_=k.dst_rows,
                                       in_offset=bass.IndirectOffsetOnAxis(ap=before_i[:, 0:1], axis=0))\
                   .then_inc(cut_in, 16)
            eng.wait_ge(rows_ready, 1)
            eng.nop(nofuse=True)
            for g in range(NG):
                for out, rows in fetches:
                    eng.indirect_dma_start(out=out[:, g, :], out_offset=None, in_=rows,
                                           in_offset=bass.IndirectOffsetOnAxis(ap=row_i[:, g:g + 1], axis=0))\
                       .then_inc(edges_in[g], 16)

        @block.vector
        def _(eng):
            done = [0]

            def link(ins):
                done[0] += 1
                ins.then_inc(vec, 1)
                eng.wait_ge(vec, done[0])

            eng.memset(ones[:], 1.0).then_inc(ones_done, 1)
            link(eng.memset(k.dloc_p[:, NS:], -1.0))
            link(eng.memset(k.w_p[:, NS:], 0.0))
            eng.wait_ge(const_done, 5)
            link(eng.tensor_scalar(tri_ge[:], diff[:], 0.0, None, ALU.is_ge))
            link(eng.tensor_scalar(tri_gt[:], diff[:], 0.0, None, ALU.is_gt))
            if layer == 0:
                eng.wait_ge(dst_in, 16)
                link(eng.tensor_copy(row_last[:], dst_all[:, :, P - 1]))
                link(eng.tensor_scalar(less[:], bound_row[:], row_last[:, 0:1], None, ALU.is_gt))
                for c in range(1, CR):
                    ins = eng.scalar_tensor_tensor(out=less[:], in0=bound_row[:], scalar=row_last[:, c:c + 1],
                                                   in1=less[:], op0=ALU.is_gt, op1=ALU.add)
                    if c < CR - 1:
                        link(ins)
                    else:
                        ins.then_inc(less_ready, 1)
                eng.wait_ge(before_mm, 1)
                link(eng.tensor_scalar(before[:], ps_small[0:NB, 0:1], float(ROWS - 1), None, ALU.min))
                eng.tensor_copy(before_i[:], before[:]).then_inc(before_ready, 1)
                eng.wait_ge(cut_in, 16)
                link(eng.tensor_copy(cut[:], cut_i[:]))
                link(eng.tensor_scalar(cut_lt[:], cut[:], bound_col[:, 0:1], None, ALU.is_lt))
                link(eng.tensor_reduce(inside[:], cut_lt[:], AX.X, ALU.add))
            else:
                link(eng.tensor_scalar(before_i[:], k.bucket_start[:], 1.0 / P, None, ALU.mult))
                link(eng.tensor_copy(before[:], before_i[:]))
                link(eng.scalar_tensor_tensor(out=inside[:], in0=before[:], scalar=-float(P), in1=k.bucket_start[:],
                                              op0=ALU.mult, op1=ALU.add))
                link(eng.tensor_scalar(cut_lt[:, 0:1], inside[:], 0.0, None, ALU.is_lt))
                link(eng.tensor_tensor(before[:], before[:], cut_lt[:, 0:1], ALU.subtract))
                link(eng.scalar_tensor_tensor(out=inside[:], in0=cut_lt[:, 0:1], scalar=float(P), in1=inside[:],
                                              op0=ALU.mult, op1=ALU.add))
            link(eng.tensor_scalar(first[:], inside[:], float(P), before[:, 0:1], ALU.is_ge, ALU.add))
            link(eng.tensor_scalar(last[:], inside[:], 0.0, before[:, 0:1], ALU.is_gt, ALU.add))
            link(eng.tensor_scalar(nfirst[:], first[:], -1.0, None, ALU.mult))
            link(eng.memset(jump[:, 0:1], 1.0))
            eng.tensor_tensor(jump[:, 1:2], first[:], last[:], ALU.subtract).then_inc(ends_ready, 1)
            eng.wait_ge(start_mm, 1)
            link(eng.tensor_copy(start[:], ps_small[0:NB, 1:2]))
            eng.tensor_scalar(reached[:], step_row[:], start[:, 0:1], None, ALU.is_ge).then_inc(reached_ready, 1)
            eng.wait_ge(steps_mm, 1)
            steps = ps_small[0:SG, 128:128 + 2 * NG].rearrange("p (g c) -> p g c", c=2)
            link(eng.tensor_scalar(k.tile_of[:], steps[:, :, 0], -1.0, None, ALU.add))
            link(eng.tensor_tensor(row_f[:], steps[:, :, 1], step_of[:], ALU.add))
            eng.tensor_scalar(row_i[:], row_f[:], float(ROWS - 1), None, ALU.min).then_inc(rows_ready, 1)
            link(eng.tensor_scalar(ntile_col[:], k.tile_of[:], -float(P), None, ALU.mult))
            for c in range(NS // RC):
                eng.wait_ge(rows_mm, c + 1)
                link(eng.tensor_scalar(k.tile_col[0:1, c * RC:(c + 1) * RC], ps_row[0:1, c, 0:RC], -1.0, None,
                                       ALU.add))
            for g in range(NG):
                eng.wait_ge(edges_in[g], 16 * len(fetches))
                if g >= 2:
                    eng.wait_ge(turned, g - 1)
                eng.tensor_copy(src_f[:, g % 2, :], src_g[:, g, :])
                eng.tensor_copy(w_f[:, g % 2, :], w_g[:, g, :])
                eng.tensor_scalar(dst_f[:, g % 2, :], dst_g[:, g, :], ntile_col[:, g:g + 1], None, ALU.add)\
                   .then_inc(edges_f, 1)
                eng.wait_ge(turned, g + 1)
                for n, out in enumerate((k.src_p, k.dloc_p, k.w_p)):
                    eng.tensor_copy(out[:, g * SG:(g + 1) * SG], ps_t[0:P, n, (g % 2) * 256:(g % 2) * 256 + SG])\
                       .then_inc(laid, 1)

        @block.tensor
        def _(eng):
            if layer == 0:
                eng.wait_ge(less_ready, 1)
                eng.wait_ge(ones_done, 1)
                eng.matmul(ps_small[0:NB, 0:1], less[:], ones[0:NT, :], start=True, stop=True).then_inc(before_mm, 1)
            eng.wait_ge(ends_ready, 1)
            eng.matmul(ps_small[0:NB, 1:2], tri_ge[:], last[:], start=True, stop=False)
            eng.matmul(ps_small[0:NB, 1:2], tri_gt[:], nfirst[:], start=False, stop=True).then_inc(start_mm, 1)
            eng.wait_ge(reached_ready, 1)
            for g in range(NG):
                mm = eng.matmul(ps_small[0:SG, 128 + 2 * g:130 + 2 * g], reached[:, g * SG:(g + 1) * SG], jump[:],
                                start=True, stop=True)
            mm.then_inc(steps_mm, 1)
            for c in range(NS // RC):
                eng.matmul(ps_row[0:1, c, 0:RC], jump[:, 0:1], reached[:, c * RC:(c + 1) * RC],
                           start=True, stop=True).then_inc(rows_mm, 1)
            for g in range(NG):
                eng.wait_ge(edges_f, g + 1)
                if g >= 2:
                    eng.wait_ge(laid, 3 * (g - 1))
                for n, tile in enumerate((src_f, dst_f, w_f)):
                    mm = eng.transpose(ps_t[0:P, n, (g % 2) * 256:(g % 2) * 256 + SG], tile[:, g % 2, :],
                                       k.ident[0:SG, 0:SG])
                mm.then_inc(turned, 1)


def degrees_and_key_max(nc, k):
    with ExitStack() as ctx:
        sb, pb, sem = allocators(nc, ctx, "deg")
        wk = sb("wk", [128, 2, D])
        lane16 = sb("lane16", [P, 128], BF16)
        neg_half = sb("neg_half", [P, TS])
        xt = sb("x_tiles", [P, TS, D])
        st = sb("stats", [P, TS, 6])
        mv = sb("mean_var", [P, TS, 2])
        ve = sb("var_eps", [P, TS])
        rs = sb("rstd_now", [P, TS])
        xn = sb("xn_tiles", [P, TS, D])
        xnT = sb("xnT", [128, 2, 2, P])
        kmax = sb("kmax_rows", [P, D])
        dl = sb("dloc_now", [P, STEPS])
        hot = sb("hot", [P, 2, GRP, 128], BF16)
        ws = sb("w_split", [P, STEPS, 3], BF16)
        wr = sb("w_rest", [P, 2, STEPS])
        hot_hi = sb("hot_hi", [P, k.RPS, 10], BF16)
        hot_lo = sb("hot_lo", [P, k.RPS, 10], BF16)
        zeros = sb("b_zeros", [P, 40], BF16)
        ps_T = [pb(f"ps_T{n}", [128, 2, P]) for n in range(2)]
        ps_k = [pb(f"ps_k{n}", [P, D]) for n in range(2)]
        ps_deg = [pb(f"ps_deg{n}", [128, STEPS // 2, 3]) for n in range(2)]
        ps_hist = pb("ps_hist", [10, 4, 10])

        w_in = sem("wk_in")
        x_in = [sem(f"x_in{j}") for j in range(TS)]
        consts = sem("b_consts")
        x_free = sem("x_free")
        stats = sem("b_stats")
        aggr = sem("b_aggr")
        rstd_steps = sem("rstd_steps")
        rstd_ready = sem("rstd_ready")
        rstd_used = sem("rstd_used")
        mv_free = sem("mv_free")
        xn_ready = sem("xn_ready")
        T_done = sem("T_done")
        xnT_ready = sem("xnT_ready")
        k_done = sem("k_done")
        kmax_done = sem("kmax_done")
        dl_ready = sem("dl_ready")
        hot_ready = sem("hot_ready")
        deg_done = sem("deg_done")
        split_steps = sem("split_steps")
        split_ready = sem("split_ready")
        deg_kept = sem("deg_kept")
        digits_ready = sem("digits_ready")
        hist_done = sem("hist_done")
        hist_zero = sem("hist_zero")
        block = ctx.enter_context(nc.Block())

        @block.sync
        def _(eng):
            eng.dma_start(wk[:, :, :], k.L0_mix_Wqkv[:, D:2 * D].rearrange("(c p) n -> p c n", c=2)).then_inc(w_in, 16)
            with eng.Fori(0, k.NSUP) as i:
                for j in range(TS):
                    eng.wait_ge(x_free, i * TS + j + 1)
                    eng.dma_start(xt[:, j, :], k.x[bass.ds(i * (P * TS) + j * P, P), :]).then_inc(x_in[j], 16)

        @block.gpsimd
        def _(eng):
            eng.memset(neg_half[:], -0.5).then_inc(consts, 1)
            eng.sem_inc(mv_free, 1)
            eng.wait_ge(consts, 2)
            with eng.Fori(0, k.NSUP) as i:
                eng.wait_ge(deg_done, i * GRPS + 2)
                eng.nop(nofuse=True)
                w = k.w_p[:, bass.ds(i * STEPS, STEPS)]
                eng.tensor_copy(ws[:, :, 0], w).then_inc(split_steps, 1)
                eng.wait_ge(split_steps, i * 4 + 1)
                eng.nop(nofuse=True)
                eng.tensor_tensor(wr[:, 0, :], w, ws[:, :, 0], ALU.subtract).then_inc(split_steps, 1)
                eng.wait_ge(split_steps, i * 4 + 2)
                eng.nop(nofuse=True)
                eng.tensor_copy(ws[:, :, 1], wr[:, 0, :]).then_inc(split_steps, 1)
                eng.wait_ge(split_steps, i * 4 + 3)
                eng.nop(nofuse=True)
                eng.tensor_tensor(wr[:, 1, :], wr[:, 0, :], ws[:, :, 1], ALU.subtract).then_inc(split_steps, 1)
                eng.wait_ge(split_steps, i * 4 + 4)
                eng.nop(nofuse=True)
                eng.tensor_copy(ws[:, :, 2], wr[:, 1, :]).then_inc(split_ready, 1)
                eng.wait_ge(aggr, i + 1)
                eng.nop(nofuse=True)
                eng.tensor_scalar(ve[:], mv[:, :, 1], LN_EPS, None, ALU.add).then_inc(rstd_steps, 1)
                eng.wait_ge(rstd_steps, i + 1)
                eng.wait_ge(rstd_used, i + 1)
                eng.nop(nofuse=True)
                eng.tensor_tensor(rs[:], ve[:], neg_half[:], ALU.pow).then_inc(rstd_ready, 1)
                eng.tensor_copy(k.mean[:, bass.ds(i * TS, TS)], mv[:, :, 0])
                eng.wait_ge(rstd_ready, i + 1)
                eng.nop(nofuse=True)
                eng.tensor_copy(k.rstd[:, bass.ds(i * TS, TS)], rs[:]).then_inc(mv_free, 1)

        @block.vector
        def _(eng):
            eng.tensor_copy(lane16[:], k.lane[0:P, :]).then_inc(consts, 1)
            eng.memset(zeros[:], 0.0).then_inc(hist_zero, 1)
            eng.memset(kmax[:], -3.0e38).then_inc(kmax_done, 2)
            eng.sem_inc(x_free, TS)
            eng.sem_inc(rstd_used, 1)
            eng.sem_inc(deg_kept, 2)
            eng.sem_inc(dl_ready, 1)
            eng.wait_ge(consts, 2)

            def one_hots(i, g):
                eng.wait_ge(deg_done, i * GRPS + g + 1)
                for l in range(GRP):
                    ins = eng.tensor_scalar(hot[:, g % 2, l, :], lane16[:], dl[:, g * GRP + l:g * GRP + l + 1], None,
                                            ALU.is_equal)
                ins.then_inc(hot_ready, 1)

            def keep(i, half):
                eng.wait_ge(deg_done, i * GRPS + (half + 1) * (GRPS // 2) + 2)
                eng.tensor_reduce(k.deg_step[:, bass.ds(i * STEPS + half * (STEPS // 2), STEPS // 2)],
                                  ps_deg[half][:, :, :], AX.X, ALU.add).then_inc(deg_kept, 1)

            with eng.Fori(0, k.NSUP) as i:
                eng.tensor_copy(dl[:], k.dloc_p[:, bass.ds(i * STEPS, STEPS)]).then_inc(dl_ready, 1)
                for j in range(TS):
                    eng.wait_ge(x_in[j], i * 16 + 16)
                    eng.bn_stats(st[:, j, :], xt[:, j, :]).then_inc(stats, 1)
                eng.wait_ge(stats, i * TS + TS)
                eng.wait_ge(mv_free, i + 1)
                eng.nop(nofuse=True)
                for j in range(TS):
                    ins = eng.bn_aggr(mv[:, j, :], st[:, j, :])
                ins.then_inc(aggr, 1)
                eng.wait_ge(dl_ready, i + 2)
                one_hots(i, 0)
                one_hots(i, 1)
                eng.wait_ge(hist_done, i + 1)
                for hot_d, digit in ((hot_hi, k.digit_hi), (hot_lo, k.digit_lo)):
                    eng.tensor_tensor(hot_d[:, :, :],
                                      lane16[:, 0:10].unsqueeze(1).to_broadcast([P, k.RPS, 10]),
                                      digit[:, bass.ds(i * k.RPS, k.RPS)].unsqueeze(2).to_broadcast([P, k.RPS, 10]),
                                      ALU.is_equal).then_inc(digits_ready, 1)
                for j in range(TS):
                    if j == 0:
                        eng.wait_ge(rstd_ready, i + 1)
                    eng.wait_ge(T_done, i * TS + j + 1)
                    ins = eng.tensor_scalar(xn[:, j, :], xt[:, j, :], mv[:, j, 0:1], rs[:, j:j + 1],
                                            ALU.subtract, ALU.mult)
                    ins.then_inc(xn_ready, 1)
                    eng.wait_ge(xn_ready, i * TS + j + 1)
                    eng.sem_inc(x_free, 1)
                eng.sem_inc(rstd_used, 1)
                for j in range(TS):
                    one_hots(i, 2 + 2 * j)
                    one_hots(i, 3 + 2 * j)
                    eng.wait_ge(k_done, i * TS + j + 3)
                    eng.wait_ge(kmax_done, i * TS + j + 2)
                    eng.tensor_tensor(kmax[:], kmax[:], ps_k[j % 2][:, :], ALU.max).then_inc(kmax_done, 1)
                    if j == 2:
                        keep(i, 0)
                one_hots(i, 10)
                one_hots(i, 11)
                keep(i, 1)
            eng.wait_ge(kmax_done, 2 + TS * k.NSUP)
            eng.tensor_copy(k.key_max[:], kmax[:])
            eng.wait_ge(hist_done, 1 + k.NSUP)
            eng.tensor_copy(k.hist[:, :, :], ps_hist[:, :, :])

        @block.scalar
        def _(eng):
            eng.sem_inc(xnT_ready, 2)
            with eng.Fori(0, k.NSUP) as i:
                for j in range(TS):
                    eng.wait_ge(T_done, i * TS + j + TS + 1)
                    eng.wait_ge(k_done, i * TS + j + 1)
                    eng.copy(xnT[:, j % 2, :, :], ps_T[j % 2][:, :, :]).then_inc(xnT_ready, 1)

        @block.tensor
        def _(eng):
            eng.sem_inc(T_done, TS)
            eng.sem_inc(k_done, 2)
            eng.sem_inc(deg_done, 2)

            def degrees(i, g):
                if g == 0:
                    eng.wait_ge(split_ready, i + 1)
                eng.wait_ge(hot_ready, i * GRPS + g + 1)
                if g % (GRPS // 2) == 0:
                    eng.wait_ge(deg_kept, i * 2 + g // (GRPS // 2) + 1)
                half, at = divmod(g * GRP, STEPS // 2)
                for l in range(GRP):
                    mm = eng.matmul(ps_deg[half][:, at + l, :], hot[:, g % 2, l, :], ws[:, g * GRP + l, :],
                                    start=True, stop=True)
                mm.then_inc(deg_done, 1)

            def turn(i, j):
                eng.wait_ge(xn_ready, i * TS + j + 1)
                eng.wait_ge(xnT_ready, i * TS + j + 1)
                for c in range(2):
                    mm = eng.transpose(ps_T[j % 2][:, c, :], xn[:, j, c * H2:(c + 1) * H2], k.ident[0:P, 0:P])
                mm.then_inc(T_done, 1)

            def keys(i, j):
                eng.wait_ge(xnT_ready, i * TS + j + 3)
                eng.wait_ge(kmax_done, i * TS + j + 1)
                for c in range(2):
                    mm = eng.matmul(ps_k[j % 2][:, :], xnT[:, j % 2, c, :], wk[:, c, :], start=(c == 0), stop=(c == 1))
                mm.then_inc(k_done, 1)

            eng.wait_ge(w_in, 16)
            eng.wait_ge(hist_zero, 1)
            eng.matmul(ps_hist[:, :, :], zeros[:, 0:10], zeros[:], start=True, stop=False,
                       skip_group_check=True).then_inc(hist_done, 1)
            with eng.Fori(0, k.NSUP) as i:
                degrees(i, 0)
                degrees(i, 1)
                turn(i, 0)
                for j in range(TS):
                    if j + 1 < TS:
                        turn(i, j + 1)
                    keys(i, j)
                    degrees(i, 2 + 2 * j)
                    degrees(i, 3 + 2 * j)
                degrees(i, 10)
                degrees(i, 11)
                eng.wait_ge(digits_ready, i * 2 + 2)
                for r in range(k.RPS):
                    mm = eng.matmul(ps_hist[:, r % 4, :], hot_hi[:, r, :], hot_lo[:, r, :], start=False, stop=False,
                                    skip_group_check=True)
                mm.then_inc(hist_done, 1)


def degree_scales(nc, k):
    NG = k.NS // SG
    with ExitStack() as ctx:
        sb, pb, sem = allocators(nc, ctx, "scale")
        deg_T = sb("deg_T", [SG, 2, 128])
        tile_hot = sb("tile_hot", [SG, NG, k.NT])
        degs = sb("degs", [k.NT, P])
        neg_half = sb("neg_half2", [k.NT, P])
        dinv_T = sb("dinv_T", [k.NT, P])
        kcol = sb("kcol", [128, 2])
        krow = sb("krow", [1, D])
        ones = sb("ones_row", [1, P])
        ps_t = [pb(f"ps_degT{n}", [SG, 128]) for n in range(2)]
        ps_deg = pb("ps_degs", [k.NT, P])
        ps_dinv = pb("ps_dinv", [P, k.NT])
        ps_k = pb("ps_kT", [128, 2, P])
        ps_row_bounds = pb("ps_krow", [128, D + 8])
        ps_row = ps_row_bounds[0:1, 0:D]
        ps_b = pb("ps_kb", [P, D])
        spread = sb("spread", [10, 4, 10, 10])
        ones10 = sb("ones10", [10, P])
        counts = sb("counts", [P, 4, 100])
        total = sb("total", [P, 100])
        incl = sb("incl", [P, 100])
        zero_row = sb("zero_row", [P, 100])
        bounds = sb("bounds", [1, k.NT + 1])
        ps_cnt = pb("ps_cnt", [P, 4, 100])
        ps_bounds = ps_row_bounds[0:k.NT + 1, D:D + 1]
        consts, hot_ready, turned, kept, deg_used, degs_ready, dinv_ready, dinv_mm, chain = (
            sem(n) for n in ("b2_consts", "tile_hot_ready", "deg_turned", "deg_kept2", "deg_used", "degs_ready",
                             "dinv_ready", "dinv_mm", "b2_chain"))
        spread_ready, cnt_mm, bounds_ready, bounds_mm = (
            sem(n) for n in ("spread_ready", "cnt_mm", "bounds_ready", "bounds_mm"))
        kT_done, kcol_ready, krow_mm, krow_ready, kb_mm = (
            sem(n) for n in ("kT_done", "kcol_ready", "krow_mm", "krow_ready", "kb_mm"))
        block = ctx.enter_context(nc.Block())

        @block.gpsimd
        def _(eng):
            eng.memset(neg_half[:], -0.5).then_inc(consts, 1)
            eng.memset(ones[:], 1.0).then_inc(consts, 1)
            eng.wait_ge(consts, 2)
            eng.wait_ge(degs_ready, 1)
            eng.tensor_tensor(dinv_T[:], degs[:], neg_half[:], ALU.pow).then_inc(dinv_ready, 1)

        @block.vector
        def _(eng):
            done = [0]

            def link(ins):
                done[0] += 1
                ins.then_inc(chain, 1)
                eng.wait_ge(chain, done[0])

            link(eng.memset(ones10[:], 1.0))
            for q in range(4):
                ins = eng.tensor_tensor(spread[:, q, :, :],
                                        k.hist[:, q, :].unsqueeze(1).to_broadcast([10, 10, 10]),
                                        k.ident[0:10, 0:10].unsqueeze(2).to_broadcast([10, 10, 10]), ALU.mult)
            ins.then_inc(spread_ready, 1)
            link(eng.memset(zero_row[:], 0.0))
            eng.wait_ge(cnt_mm, 1)
            link(eng.tensor_copy(counts[:, :, :], ps_cnt[:, :, :]))
            link(eng.tensor_tensor(total[:], counts[:, 0, :], counts[:, 1, :], ALU.add))
            link(eng.tensor_tensor(total[:], total[:], counts[:, 2, :], ALU.add))
            link(eng.tensor_tensor(total[:], total[:], counts[:, 3, :], ALU.add))
            link(eng.tensor_tensor_scan(incl[:], total[:], zero_row[:], 0.0, ALU.add, ALU.add))
            link(eng.tensor_tensor(k.rank_start[:, 0, :], incl[:], total[:], ALU.subtract))
            for q in range(1, 4):
                link(eng.tensor_tensor(k.rank_start[:, q, :], k.rank_start[:, q - 1, :], counts[:, q - 1, :], ALU.add))
            link(eng.memset(bounds[:], float(P * k.ROWS)))
            eng.tensor_copy(bounds[0:1, 0:k.NT], k.rank_start[0:1, 0, 0:k.NT]).then_inc(bounds_ready, 1)
            eng.wait_ge(bounds_mm, 1)
            link(eng.tensor_copy(k.bucket_start[:], ps_bounds))
            eng.wait_ge(kT_done, 1)
            eng.tensor_reduce(kcol[:], ps_k[:, :, :], AX.X, ALU.max).then_inc(kcol_ready, 1)
            for g in range(NG):
                eng.tensor_scalar(tile_hot[:, g, :], k.lane[0:SG, 0:k.NT], k.tile_of[:, g:g + 1], None,
                                  ALU.is_equal).then_inc(hot_ready, 1)
            eng.wait_ge(krow_mm, 1)
            eng.tensor_copy(krow[:], ps_row).then_inc(krow_ready, 1)
            eng.wait_ge(deg_used, NG)
            eng.tensor_scalar(degs[:], ps_deg[:, :], 1.0, None, ALU.add).then_inc(degs_ready, 1)
            eng.wait_ge(dinv_mm, 1)
            link(eng.tensor_copy(k.dinv[:], ps_dinv[:, :]))
            link(eng.tensor_tensor(k.scale0[:], k.dinv[:], k.rstd[:], ALU.mult))
            eng.wait_ge(kb_mm, 1)
            link(eng.tensor_copy(k.key_max[:], ps_b[:, :]))

        @block.scalar
        def _(eng):
            for g in range(NG):
                eng.wait_ge(turned, g + 1)
                if g >= 2:
                    eng.wait_ge(deg_used, g - 1)
                eng.copy(deg_T[:, g % 2, :], ps_t[g % 2][:, :]).then_inc(kept, 1)

        @block.tensor
        def _(eng):
            for c in range(2):
                mm = eng.transpose(ps_k[:, c, :], k.key_max[:, c * H2:(c + 1) * H2], k.ident[0:P, 0:P])
            mm.then_inc(kT_done, 1)
            eng.wait_ge(spread_ready, 1)
            eng.matmul(ps_cnt[:, :, :], ones10[:], spread[:, :, :, :], start=True, stop=True).then_inc(cnt_mm, 1)
            eng.wait_ge(bounds_ready, 1)
            eng.transpose(ps_bounds, bounds[0:1, :], k.ident[0:1, 0:1]).then_inc(bounds_mm, 1)
            eng.wait_ge(kcol_ready, 1)
            for c in range(2):
                mm = eng.transpose(ps_row[:, c * H2:(c + 1) * H2], kcol[:, c:c + 1], k.ident[:, :])
            mm.then_inc(krow_mm, 1)
            eng.wait_ge(krow_ready, 1)
            eng.wait_ge(consts, 2)
            eng.matmul(ps_b[:, :], ones[:], krow[:], start=True, stop=True).then_inc(kb_mm, 1)

            def turn(g):
                if g >= 2:
                    eng.wait_ge(kept, g - 1)
                eng.transpose(ps_t[g % 2][:, :], k.deg_step[:, g * SG:(g + 1) * SG], k.ident[:, :]).then_inc(turned, 1)

            turn(0)
            for g in range(NG):
                if g + 1 < NG:
                    turn(g + 1)
                eng.wait_ge(kept, g + 1)
                eng.wait_ge(hot_ready, g + 1)
                mm = eng.matmul(ps_deg[:, :], tile_hot[:, g, :], deg_T[:, g % 2, 0:P], start=(g == 0),
                                stop=(g == NG - 1))
                mm.then_inc(deg_used, 1)
            eng.wait_ge(dinv_ready, 1)
            eng.transpose(ps_dinv[:, :], dinv_T[:], k.ident[0:k.NT, 0:k.NT]).then_inc(dinv_mm, 1)


def scale_rows(nc, k):
    DEPTH = 2
    with ExitStack() as ctx:
        sb, pb, sem = allocators(nc, ctx, "table")
        xt = sb("c_x", [P, DEPTH, TS, D])
        x_in = [sem(f"c_x_in{n}") for n in range(DEPTH)]
        out_done = [sem(f"c_out{n}") for n in range(DEPTH)]
        scaled = sem("c_scaled")
        cleared = sem("c_cleared")
        pairs, odd = divmod(k.NSUP, DEPTH)
        rows = P * TS
        block = ctx.enter_context(nc.Block())

        def place(ap, i):
            return ap[bass.ds(i * rows, rows), :].rearrange("(j p) d -> p j d", p=P)

        def turns(eng, run):
            for n in range(DEPTH):
                run(n, n, 0)
            with eng.Fori(1, pairs) as m:
                for n in range(DEPTH):
                    run(m * DEPTH + n, n, m)
            for n in range(odd):
                run(k.NSUP - odd + n, n, pairs)

        @block.sync
        def _(eng):
            def load(i, n, turn):
                if not (isinstance(turn, int) and turn == 0):
                    eng.wait_ge(out_done[n], turn * 16)
                eng.dma_start(xt[:, n, :, :], place(k.x, i)).then_inc(x_in[n], 16)

            turns(eng, load)

        @block.scalar
        def _(eng):
            def store(i, n, turn):
                eng.wait_ge(scaled, i * TS + TS)
                eng.dma_start(place(k.table0, i), xt[:, n, :, :]).then_inc(out_done[n], 16)

            turns(eng, store)
            for n in range(DEPTH):
                eng.wait_ge(out_done[n], 16 * (pairs + (n < odd)))

        @block.vector
        def _(eng):
            def scale(i, n, turn):
                eng.wait_ge(x_in[n], turn * 16 + 16)
                for j in range(TS):
                    eng.tensor_scalar(xt[:, n, j, :], xt[:, n, j, :], k.mean[:, bass.ds(i * TS + j, 1)],
                                      k.scale0[:, bass.ds(i * TS + j, 1)], ALU.subtract, ALU.mult).then_inc(scaled, 1)

            turns(eng, scale)

        @block.gpsimd
        def _(eng):
            eng.memset(k.sums[:, :, :], 0.0).then_inc(cleared, 1)


class Aggregation:
    RING = 3 * GRP
    RES = 3

    def __init__(self, nc, k, sb, pb, sem, table):
        self.nc, self.k, self.table = nc, k, table
        self.idx = [sb(f"idx{n}", [P, STEPS // 2], I32) for n in range(2)]
        self.rows = sb("gathered", [P, self.RING, D])
        self.lay = sb("lay", [P, 2, GRP, P])
        self.dl = sb("dloc_now", [P, STEPS + GRP])
        self.wl = sb("w_now", [P, STEPS + GRP])
        self.res = [pb(f"agg_res{n}", [P, 1, D]) for n in range(self.RES)]
        self.idx_ready = sem("idx_ready")
        self.gathered = [sem(f"gathered{n}") for n in range(3)]
        self.lay_ready = sem("lay_ready")
        self.local_ready = sem("local_ready")
        self.multiplied = sem("multiplied")
        self.added = sem("added")

    def take_indices(self, i, half):
        eng, k = self.nc.gpsimd, self.k
        hs = STEPS // 2
        eng.wait_ge(self.multiplied, i * STEPS + half * hs + 1)
        eng.nop(nofuse=True)
        eng.tensor_copy(self.idx[half][:], k.src_p[:, bass.ds(i * STEPS + half * hs, hs)]).then_inc(self.idx_ready, 1)
        eng.wait_ge(self.idx_ready, i * 2 + half + 1)

    def gather_group(self, i, half, g):
        eng = self.nc.gpsimd
        hs = STEPS // 2
        eng.wait_ge(self.multiplied, i * STEPS + g * GRP + GRP)
        eng.nop(nofuse=True)
        for l in range(GRP):
            s = g * GRP + l
            eng.indirect_dma_start(
                out=self.rows[:, s % self.RING, :], out_offset=None, in_=self.table,
                in_offset=bass.IndirectOffsetOnAxis(ap=self.idx[half][:, s - half * hs:s - half * hs + 1], axis=0))\
               .then_inc(self.gathered[g % 3], 16)

    def gather_half(self, i, half):
        self.take_indices(i, half)
        for g in range(half * GRPS // 2, (half + 1) * GRPS // 2):
            self.gather_group(i, half, g)

    def vector_start(self):
        self.nc.vector.sem_inc(self.added, self.RES)

    def take_local(self, i, turn, first=False):
        eng, k = self.nc.vector, self.k
        if not first:
            eng.wait_ge(self.lay_ready, i * GRPS + 1)
        eng.tensor_copy(self.dl[:], k.dloc_p[:, bass.ds(i * STEPS, STEPS + GRP)]).then_inc(self.local_ready, 1)
        eng.tensor_copy(self.wl[:], k.w_p[:, bass.ds(i * STEPS, STEPS + GRP)]).then_inc(self.local_ready, 1)
        eng.wait_ge(self.local_ready, turn * 2 + 2)

    def build(self, i, g, l):
        eng, k = self.nc.vector, self.k
        s = g * GRP + l
        if l == 0:
            eng.wait_ge(self.multiplied, i * STEPS + g * GRP + self.RING - GRP)
        ins = eng.tensor_scalar(self.lay[:, g % 2, l, :], k.lane[0:P, 0:P], self.dl[:, s:s + 1], self.wl[:, s:s + 1],
                                ALU.is_equal, ALU.mult)
        if l == GRP - 1:
            ins.then_inc(self.lay_ready, 1)

    def add(self, i, g, l):
        eng, k = self.nc.vector, self.k
        s = g * GRP + l
        if l == 0:
            self.tiles = self.nc.values_load_multi_w_load_instructions(
                k.tile_col[0:1, bass.ds(i * STEPS + s, GRP)], engines=[mybir.EngineType.DVE],
                min_val=0, max_val=k.NT,
                skip_runtime_bounds_check_because="the plan gives every step a tile between 0 and the spare one")[1]
        eng.wait_ge(self.added, i * STEPS + s + self.RES)
        eng.wait_ge(self.multiplied, i * STEPS + s + self.RING + 1)
        sums = k.sums[:, bass.ds(self.tiles[l], 1), :]
        res = self.res[s % self.RES][:, :, :]
        eng.tensor_tensor(sums, sums, res, ALU.add).then_inc(self.added, 1)

    def tensor_start(self):
        self.nc.tensor.sem_inc(self.multiplied, self.RING)

    def multiply(self, i, g, half):
        eng = self.nc.tensor
        if half == 0:
            eng.wait_ge(self.lay_ready, i * GRPS + g + 1)
            eng.wait_ge(self.gathered[g % 3], (i * (GRPS // 3) + g // 3 + 1) * 16 * GRP)
        for l in range(half * GRP // 2, (half + 1) * GRP // 2):
            s = g * GRP + l
            eng.wait_ge(self.added, i * STEPS + s + 1)
            eng.matmul(self.res[s % self.RES][:, 0, :], self.lay[:, g % 2, l, :],
                       self.rows[:, s % self.RING, :], start=True, stop=True).then_inc(self.multiplied, 1)


def spans(n):
    return [range(h * n // (2 * GRPS), (h + 1) * n // (2 * GRPS)) for h in range(2 * GRPS)]


def sum_layer0(nc, k):
    NB4 = k.RPS // 4

    def slot(b):
        return 2 if NB4 % 2 and b == NB4 - 1 else b % 2

    with ExitStack() as ctx:
        sb, pb, sem = allocators(nc, ctx, "sum0")
        agg = Aggregation(nc, k, sb, pb, sem, k.table0)
        wk = sb("wk", [128, 2, D])
        xt = sb("x_tiles", [P, TS, D])
        xn = sb("xn_tiles", [P, TS, D + 1])
        xnT = sb("xnT", [128, 2, P])
        kd = sb("key_less_max", [P, D])
        ek = sb("exp_key", [P, D])
        zeros = sb("d_zeros", [P, D + 1])
        lane16 = sb("lane16", [P, 100], BF16)
        lower = sb("edges_before", [P, P], BF16)
        upper = sb("edges_after", [P, P], BF16)
        tri = sb("tri", [P, P])
        hot = sb("src_hot", [P, 3, 4, 100], BF16)
        junk = sb("junk", [P, 4, 100])
        rank = sb("rank_now", [P, k.RPS])
        pos = sb("pos", [P, k.RPS], I32)
        ps_T = pb("ps_T", [128, 2, P])
        ps_k = pb("ps_k", [P, D])
        ps_ctx = [pb(f"ps_ctx{c}", [128, D + 1]) for c in range(2)]
        ps_rank = pb("ps_rank", [P, 4, 100])

        pos_out = sem("pos_out")
        x_in = [sem(f"x_in{j}") for j in range(TS)]
        x_free, xn_ready, T_done, xnT_ready, k_done, kd_ready, ek_ready, ctx_done = (
            sem(n) for n in ("x_free", "xn_ready", "T_done", "xnT_ready", "k_done", "kd_ready", "ek_ready", "ctx_done"))
        hot_ready, pre_done, ranked, rest_done, rank_kept, consts, tri_ready, zeros_ready = (
            sem(n) for n in ("src_hot_ready", "pre_done", "ranked", "rest_done", "rank_kept", "d_consts", "tri_ready",
                             "zeros_ready"))
        block = ctx.enter_context(nc.Block())

        @block.sync
        def _(eng):
            eng.dma_start(wk[:, :, :], k.L0_mix_Wqkv[:, D:2 * D].rearrange("(c p) n -> p c n", c=2)).then_inc(pos_out, 16)
            with eng.Fori(0, k.NSUP) as i:
                for j in range(TS):
                    eng.wait_ge(x_free, i * TS + j + 1)
                    eng.dma_start(xt[:, j, :], k.x[bass.ds(i * (P * TS) + j * P, P), :]).then_inc(x_in[j], 16)
                eng.wait_ge(rank_kept, i + 2)
                eng.dma_start(k.pos_d[:, bass.ds(i * k.RPS, k.RPS)], pos[:]).then_inc(pos_out, 16)
            eng.wait_ge(pos_out, 16 + 16 * k.NSUP)

        @block.gpsimd
        def _(eng):
            eng.iota(tri[:], [[1, P]], base=0, channel_multiplier=-1,
                     allow_small_or_imprecise_dtypes=True).then_inc(tri_ready, 1)
            with eng.Fori(0, k.NSUP) as i:
                agg.gather_half(i, 0)
                agg.gather_half(i, 1)

        @block.vector
        def _(eng):
            agg.vector_start()
            eng.memset(zeros[:, :], 0.0).then_inc(zeros_ready, 1)
            eng.memset(xn[:, :, D:D + 1], 1.0).then_inc(consts, 1)
            eng.tensor_copy(lane16[:], k.lane[0:P, 0:100]).then_inc(consts, 1)
            eng.wait_ge(tri_ready, 1)
            eng.tensor_scalar(lower[:], tri[:], 0.0, None, ALU.is_gt).then_inc(consts, 1)
            eng.tensor_scalar(upper[:], tri[:], 0.0, None, ALU.is_le).then_inc(consts, 1)
            eng.wait_ge(consts, 4)
            eng.sem_inc(x_free, TS)
            eng.sem_inc(kd_ready, 1)
            eng.sem_inc(rank_kept, 1)

            def source_hots(i, b):
                eng.wait_ge(rest_done, i * NB4 + b + 1)
                eng.tensor_tensor(hot[:, slot(b), :, :],
                                  lane16[:].unsqueeze(1).to_broadcast([P, 4, 100]),
                                  k.src_tile[:, bass.ds(i * k.RPS + b * 4, 4)].unsqueeze(2).to_broadcast([P, 4, 100]),
                                  ALU.is_equal).then_inc(hot_ready, 1)

            def ranks(i, b):
                eng.wait_ge(pre_done, i * NB4 + b + 1)
                if b == 0:
                    eng.wait_ge(rank_kept, i + 1)
                for q in range(4):
                    ins = eng.tensor_tensor_reduce(junk[:, q, :], hot[:, slot(b), q, :], ps_rank[:, q, :], 1.0, 0.0,
                                                   ALU.mult, ALU.add, rank[:, b * 4 + q:b * 4 + q + 1])
                ins.then_inc(ranked, 1)

            agg.take_local(0, 0, first=True)
            for l in range(GRP):
                agg.build(0, 0, l)
            with eng.Fori(0, k.NSUP) as i:
                agg.take_local(i, i + 1)
                source_hots(i, 0)
                for h, batches in enumerate(spans(NB4)):
                    g = h // 2
                    j, part = divmod(h, 6)
                    t = i * TS + j
                    if part == 0:
                        eng.wait_ge(x_in[j], i * 16 + 16)
                        eng.wait_ge(ctx_done, t + 1)
                        eng.tensor_scalar(xn[:, j, 0:D], xt[:, j, :], k.mean[:, bass.ds(t, 1)], k.rstd[:, bass.ds(t, 1)],
                                          ALU.subtract, ALU.mult).then_inc(xn_ready, 1)
                        eng.wait_ge(xn_ready, t + 1)
                        eng.sem_inc(x_free, 1)
                    for l in range(h % 2 * GRP // 2, (h % 2 + 1) * GRP // 2):
                        agg.build(i, g + 1, l)
                        agg.add(i, g, l)
                    if part == 3:
                        eng.wait_ge(k_done, t + 2)
                        eng.wait_ge(ek_ready, t + 1)
                        eng.tensor_tensor(kd[:], ps_k[:, :], k.key_max[:], ALU.subtract).then_inc(kd_ready, 1)
                    for b in batches:
                        if b + 1 < NB4:
                            source_hots(i, b + 1)
                        ranks(i, b)
                eng.wait_ge(ranked, i * NB4 + NB4)
                eng.wait_ge(pos_out, i * 16 + 16)
                eng.tensor_copy(pos[:], rank[:]).then_inc(rank_kept, 1)
            for c in range(2):
                eng.wait_ge(ctx_done, TS + k.NT)
                eng.tensor_copy(k.context[:, c, :], ps_ctx[c][:, :])

        @block.scalar
        def _(eng):
            eng.sem_inc(xnT_ready, 1)
            eng.sem_inc(ek_ready, 1)
            with eng.Fori(0, k.NSUP) as i:
                for j in range(TS):
                    t = i * TS + j
                    eng.wait_ge(T_done, t + 1)
                    eng.wait_ge(k_done, t + 1)
                    eng.copy(xnT[:, :, :], ps_T[:, :, :]).then_inc(xnT_ready, 1)
                    eng.wait_ge(kd_ready, t + 2)
                    eng.wait_ge(ctx_done, t + TS)
                    eng.activation(ek[:], kd[:], ACT.Exp).then_inc(ek_ready, 1)

        @block.tensor
        def _(eng):
            agg.tensor_start()
            eng.sem_inc(k_done, 1)
            eng.sem_inc(ctx_done, TS)
            eng.sem_inc(rest_done, 2)
            eng.wait_ge(consts, 4)
            eng.matmul(ps_rank[:, :, :], k.ident[0:P, 0:P], k.rank_start[:, :, :], start=True, stop=False,
                       skip_group_check=True)

            def before(i, b):
                eng.wait_ge(hot_ready, i * NB4 + b + 1)
                for q in range(4):
                    mm = eng.matmul(ps_rank[:, q, :], lower[:], hot[:, slot(b), q, :], start=False, stop=False,
                                    skip_group_check=True)
                mm.then_inc(pre_done, 1)

            def rest(i, b):
                eng.wait_ge(ranked, i * NB4 + b + 1)
                for q in range(4):
                    mm = eng.matmul(ps_rank[:, q, :], upper[:], hot[:, slot(b), q, :], start=False, stop=False,
                                    skip_group_check=True)
                mm.then_inc(rest_done, 1)

            eng.wait_ge(pos_out, 16)
            eng.wait_ge(zeros_ready, 1)
            for c in range(2):
                eng.matmul(ps_ctx[c][:, :], zeros[:, 0:128], zeros[:, :], start=True, stop=False,
                           skip_group_check=True)
            with eng.Fori(0, k.NSUP) as i:
                for h, batches in enumerate(spans(NB4)):
                    j, part = divmod(h, 6)
                    t = i * TS + j
                    agg.multiply(i, h // 2, h % 2)
                    if part == 0:
                        eng.wait_ge(xn_ready, t + 1)
                        eng.wait_ge(xnT_ready, t + 1)
                        for c in range(2):
                            mm = eng.transpose(ps_T[:, c, :], xn[:, j, c * H2:(c + 1) * H2], k.ident[0:P, 0:P])
                        mm.then_inc(T_done, 1)
                    elif part == 2:
                        eng.wait_ge(xnT_ready, t + 2)
                        eng.wait_ge(kd_ready, t + 1)
                        for c in range(2):
                            mm = eng.matmul(ps_k[:, :], xnT[:, c, :], wk[:, c, :], start=(c == 0), stop=(c == 1))
                        mm.then_inc(k_done, 1)
                    elif part == 5:
                        eng.wait_ge(ek_ready, t + 2)
                        for c in range(2):
                            mm = eng.matmul(ps_ctx[c][:, :], ek[:, c * H2:(c + 1) * H2], xn[:, j, :],
                                            start=False, stop=False, skip_group_check=True)
                        mm.then_inc(ctx_done, 1)
                    for b in batches:
                        if b:
                            rest(i, b - 1)
                        before(i, b)
                rest(i, NB4 - 1)


def compose(nc, k, layer):
    with ExitStack() as ctx:
        sb, pb, sem = allocators(nc, ctx, f"comp{layer}")
        wv = sb("wv", [128, 2, D])
        wo = sb("wo", [128, 2, D])
        bv = sb("bv", [1, D])
        rden = sb("rden", [128, 2])
        cn = sb("context_n", [128, 2, D])
        cT = sb("context_T", [128, 2, D])
        srow = sb("key_sum_row", [1, D])
        kvT = sb("kv_T", [128, 2, 128])
        heads = sb("heads", [128, 4, 32])
        ps_t = [pb(f"ps_t{n}", [128, D]) for n in range(2)]
        ps_s = pb("ps_s", [1, D])
        ps_kv = [pb(f"ps_kv{n}", [128, 128]) for n in range(2)]
        ps_o = [pb(f"ps_o{n}", [128, D]) for n in range(2)]
        w_in, b_in, heads_ready, chain, norm_ready, turned, kept, kv_done, kv_ready, out_done = (
            sem(n) for n in ("w_in", "b_in", "heads_ready", "chain", "norm_ready", "turned", "kept", "kv_done",
                             "kv_ready", "out_done"))
        block = ctx.enter_context(nc.Block())

        @block.sync
        def _(eng):
            if layer == 0:
                eng.dma_start(wv[:, :, :], k.L0_mix_Wqkv[:, 2 * D:3 * D].rearrange("(c p) n -> p c n", c=2)).then_inc(w_in, 16)
                eng.dma_start(wo[:, :, :], k.L0_mix_Wout.rearrange("(c p) n -> p c n", c=2)).then_inc(w_in, 16)
            else:
                eng.dma_start(wv[:, :, :], k.L1_mix_Wv.rearrange("(c p) n -> p c n", c=2)).then_inc(w_in, 16)
                eng.dma_start(wo[:, :, :], k.L1_mix_Wo.rearrange("(c p) n -> p c n", c=2)).then_inc(w_in, 16)
                eng.dma_start(bv[:], k.L1_mix_bv.rearrange("(a n) -> a n", a=1)).then_inc(b_in, 16)

        @block.gpsimd
        def _(eng):
            eng.memset(heads[:, :, :], 1.0).then_inc(heads_ready, 1)
            eng.wait_ge(heads_ready, 1)
            eng.affine_select(out=heads[:, :, :], in_=heads[:, :, :], compare_op=ALU.is_ge, fill=0.0, base=0,
                              pattern=[[-32, 4], [0, 32]], channel_multiplier=1).then_inc(heads_ready, 1)
            eng.wait_ge(heads_ready, 2)
            eng.affine_select(out=heads[:, :, :], in_=heads[:, :, :], compare_op=ALU.is_ge, fill=0.0, base=31,
                              pattern=[[32, 4], [0, 32]], channel_multiplier=-1).then_inc(heads_ready, 1)
            if layer == 1:
                eng.memset(k.sums[:, :, :], 0.0)

        @block.vector
        def _(eng):
            if layer == 0:
                eng.reciprocal(rden[:], k.context[:, :, D]).then_inc(chain, 1)
                eng.wait_ge(chain, 1)
            for c in range(2):
                if layer == 0:
                    ins = eng.tensor_scalar(cn[:, c, :], k.context[:, c, 0:D], rden[:, c:c + 1], None, ALU.mult)
                else:
                    ins = eng.tensor_copy(cn[:, c, :], k.context[:, c, 0:D])
                ins.then_inc(norm_ready, 1)
            for c in range(2):
                eng.wait_ge(turned, c + 1)
                eng.tensor_copy(cT[:, c, :], ps_t[c][:, :]).then_inc(kept, 1)
            if layer == 1:
                eng.wait_ge(turned, 3)
                eng.tensor_copy(srow[:], ps_s[:, :]).then_inc(kept, 1)
            eng.wait_ge(heads_ready, 3)
            mask = heads[:, :, :].rearrange("p h c -> p (h c)")
            for c in range(2):
                eng.wait_ge(kv_done, c + 1)
                eng.tensor_tensor(kvT[:, c, :], ps_kv[c][:, :], mask, ALU.mult).then_inc(kv_ready, 1)
                if layer == 1:
                    eng.tensor_scalar(k.key_sum_of[:, c, :], mask, k.context[:, c, D:D + 1], None, ALU.mult)
            for c in range(2):
                eng.wait_ge(out_done, c + 1)
                eng.tensor_scalar(k.composed[:, c, :], ps_o[c][:, :], 32.0 ** -0.5 if layer == 0 else 1.0, None, ALU.mult)

        @block.tensor
        def _(eng):
            eng.wait_ge(norm_ready, 2)
            for m in range(2):
                for c in range(2):
                    mm = eng.transpose(ps_t[m][:, c * H2:(c + 1) * H2], cn[:, c, m * H2:(m + 1) * H2], k.ident[:, :])
                mm.then_inc(turned, 1)
            if layer == 1:
                for c in range(2):
                    mm = eng.transpose(ps_s[:, c * H2:(c + 1) * H2], k.context[:, c, D:D + 1], k.ident[:, :])
                mm.then_inc(turned, 1)
                eng.wait_ge(b_in, 16)
            eng.wait_ge(w_in, 32)
            eng.wait_ge(kept, 2 + layer)
            for c in range(2):
                for m in range(2):
                    mm = eng.matmul(ps_kv[c][:, :], wv[:, m, c * H2:(c + 1) * H2], cT[:, m, c * H2:(c + 1) * H2],
                                    start=(m == 0), stop=(m == 1 and layer == 0))
                if layer == 1:
                    mm = eng.matmul(ps_kv[c][:, :], bv[0:1, c * H2:(c + 1) * H2], srow[0:1, c * H2:(c + 1) * H2],
                                    start=False, stop=True)
                mm.then_inc(kv_done, 1)
            for c in range(2):
                eng.wait_ge(kv_ready, c + 1)
                eng.matmul(ps_o[c][:, :], kvT[:, c, :], wo[:, c, :], start=True, stop=True).then_inc(out_done, 1)


def finish_layer0(nc, k):
    TE = 2
    NP = k.NT // TE
    RPP = k.ROWS // NP
    NE = 8
    with ExitStack() as ctx:
        sb, pb, sem = allocators(nc, ctx, "fin0")
        w_gcn, w_q, w_k = (sb(n, [128, 2, D]) for n in ("w_gcn", "w_q", "w_k"))
        w_r = sb("w_router", [128, 2, NE])
        w_r_raw = sb("w_router_raw", [NE, D])
        w1 = sb("w1", [128, NE, 2, D])
        w2 = sb("w2", [128, NE, 2, D])
        b1 = sb("b1", [128, 2, NE])
        b1_raw = sb("b1_raw", [NE, D])
        b2 = sb("b2", [NE, D])
        b_gcn, half_gamma, half_beta, mix_gamma = (sb(n, [P, D]) for n in ("b_gcn", "half_gamma", "half_beta", "mix_gamma"))
        b_k = sb("b_k", [1, D])
        ones = sb("ones", [1, P])
        zeros = sb("zeros", [1, D + 1])
        neg_half = sb("neg_half", [P, TE])
        x = sb("x", [P, TE, D])
        xn = sb("xn", [P, TE, D])
        s = sb("sum_self", [P, TE, D])
        xsT = sb("xn_sum_T", [128, TE, 4, P])
        h = sb("gcn", [P, TE, D])
        q = sb("query", [P, TE, D])
        qmax, qsum, qrec = (sb(n, [P, TE, 8]) for n in ("qmax", "qsum", "qrec"))
        qT = sb("query_T", [128, TE, 2, P])
        mix = sb("mix", [P, TE, D])
        acc = sb("acc", [P, 2, TE, D])
        xt = sb("tokens", [P, TE, D])
        xtT = sb("tokens_T", [128, 2, 2, TE, P])
        hid = sb("hidden", [128, 2, 2, TE * P])
        logit = sb("logit", [P, TE, NE])
        expl = sb("exp_logit", [P, TE, NE])
        top = sb("top", [P, TE, NE])
        top_i = sb("top_i", [P, TE, NE], U32)
        top_f = sb("top_f", [P, TE, 2])
        gate = sb("gate", [P, TE, 4])
        pick = sb("pick", [P, TE, 2, NE])
        comb = sb("comb", [P, 2, TE, NE])
        combT = sb("comb_T", [NE, TE, P])
        y = sb("next_norm", [P, TE, D + 1])
        yT = sb("next_norm_T", [128, TE, 2, P])
        kexp, krelu = (sb(n, [P, TE, D]) for n in ("kexp", "krelu"))
        st = sb("stats", [P, 4, TE, 6])
        mv = sb("mean_var", [P, 4, TE, 2])
        ve = sb("var_eps", [P, 4, TE])
        rs = sb("rstds", [P, 4, TE])
        rec = sb("rec", [P, 2, RPP, 3], I32)
        pos = sb("pos", [P, 2, RPP], I32)
        ps_up = [pb(f"ps_up{n}", [128, TE * P]) for n in range(2)]
        ps_dn = [pb(f"ps_dn{n}", [P, D]) for n in range(2)]
        ps_T = pb("ps_T", [128, 4, P])
        ps_M = pb("ps_M", [P, D])
        ps_ctx = [pb(f"ps_ctx{c}", [128, D + 1]) for c in range(2)]
        LN_X2, LN_H, LN_MIX, LN_X1 = range(4)

        w_in = sem("w_in")
        e_in = sem("e_in")
        st_done, mv_ready, rs_steps, rs_ready = ([sem(f"{name}{w}") for w in range(4)]
                                                 for name in ("st_done", "mv_ready", "rs_steps", "rs_ready"))
        x_in = [sem(f"x_in{j}") for j in range(TE)]
        rec_in = [sem(f"rec_in{n}") for n in range(2)]
        scattered = [sem(f"scattered{n}") for n in range(2)]
        out_done = [sem(f"out_done{j}") for j in range(TE)]
        names = ("setup", "power_ready", "k_below", "k_exp", "share_done", "setup_mm", "consts", "x_free", "xs_ready",
                 "T_done", "T_kept", "h_done", "h_kept", "q_done", "q_kept", "q_exp", "qn_ready", "qT_done",
                 "qT_kept", "mix_done", "mix_kept", "xt_ready", "xT_done", "xT_kept", "r_done", "r_kept", "r_exp",
                 "comb_ready", "cT_done", "cT_kept", "b2_done", "acc_ready", "up_done", "up_kept", "dn_done",
                 "dn_kept", "y_ready", "yT_done", "yT_kept", "k_done", "k_kept", "phi_ready", "ctx_done", "h_chain",
                 "q_chain", "m_chain", "r_chain", "xt_added")
        S = Shared()
        (S.setup, S.power_ready, S.k_below, S.k_exp, S.share_done, S.setup_mm, S.consts, S.x_free, S.xs_ready,
         S.T_done, S.T_kept, S.h_done, S.h_kept, S.q_done, S.q_kept, S.q_exp, S.qn_ready, S.qT_done, S.qT_kept,
         S.mix_done, S.mix_kept, S.xt_ready, S.xT_done, S.xT_kept, S.r_done, S.r_kept, S.r_exp, S.comb_ready,
         S.cT_done, S.cT_kept, S.b2_done, S.acc_ready, S.up_done, S.up_kept, S.dn_done, S.dn_kept, S.y_ready,
         S.yT_done, S.yT_kept, S.k_done, S.k_kept, S.phi_ready, S.ctx_done, S.h_chain, S.q_chain, S.m_chain,
         S.r_chain, S.xt_added) = (sem(n) for n in names)
        block = ctx.enter_context(nc.Block())

        def chunk(n):
            if n < 2:
                return "up", 0, n
            e, c = divmod(n - 2, 4)
            if e == NE - 1:
                return "down", e, c
            return ("up", e + 1, c) if c < 2 else ("down", e, c - 2)

        def pipeline(eng, run):
            run(0, 0, 0, moe=False, back=False)
            run(0, 0, 0, back=False)
            with eng.Fori(0, (NP - 2) // 2) as m:
                run(m * 2 + 1, 1, m)
                run(m * 2 + 2, 0, m + 1)
            run(NP - 1, (NP - 1) % 2, (NP - 1) // 2, front=False)
            run(NP, NP % 2, NP // 2, front=False, moe=False)

        @block.sync
        def _(eng):
            def row(ap, n):
                return ap.rearrange("(a n) -> a n", a=1).to_broadcast([n, D])

            half = "(c p) n -> p c n"
            eng.dma_start(w_gcn[:, :, :], k.L0_gnn_W.rearrange(half, c=2)).then_inc(w_in, 16)
            eng.dma_start(w_q[:, :, :], k.L0_mix_Wqkv[:, 0:D].rearrange(half, c=2)).then_inc(w_in, 16)
            eng.dma_start(w_r_raw[:], k.L0_ffn_router_w).then_inc(w_in, 16)
            eng.dma_start(b1_raw[:], k.L0_ffn_b1).then_inc(w_in, 16)
            eng.dma_start(b_gcn[:], row(k.L0_gnn_b, P)).then_inc(w_in, 16)
            eng.dma_start(half_gamma[:], row(k.L0_gnn_gamma, P)).then_inc(w_in, 16)
            eng.dma_start(half_beta[:], row(k.L0_gnn_beta, P)).then_inc(w_in, 16)
            eng.dma_start(mix_gamma[:], row(k.L0_mix_gamma, P)).then_inc(w_in, 16)
            eng.dma_start(w_k[:, :, :], k.L1_mix_Wk.rearrange(half, c=2)).then_inc(out_done[0], 16)
            eng.dma_start(b2[:], k.L0_ffn_b2).then_inc(out_done[0], 16)
            eng.dma_start(b_k[:], k.L1_mix_bk.rearrange("(a n) -> a n", a=1)).then_inc(out_done[1], 16)
            eng.dma_start(w1[:, 0, :, :], k.L0_ffn_w1[0].rearrange(half, c=2)).then_inc(out_done[1], 16)
            eng.dma_start(w2[:, 0, :, :], k.L0_ffn_w2[0].rearrange(half, c=2)).then_inc(e_in, 16)
            eng.dma_start(w1[:, 1, :, :], k.L0_ffn_w1[1].rearrange(half, c=2)).then_inc(e_in, 16)
            eng.dma_start(w2[:, 1, :, :], k.L0_ffn_w2[1].rearrange(half, c=2)).then_inc(e_in, 16)
            for e in range(2, NE):
                eng.dma_start(w1[:, e, :, :], k.L0_ffn_w1[e].rearrange(half, c=2)).then_inc(e_in, 16)
                eng.dma_start(w2[:, e, :, :], k.L0_ffn_w2[e].rearrange(half, c=2)).then_inc(e_in, 16)

            def run(i, n, turn, front=True, moe=True, back=True):
                f, b = (i + 1 if moe else i), i - 1
                if front:
                    for j in range(TE):
                        if moe:
                            eng.wait_ge(S.h_chain, f * 10 - 1 + j)
                        eng.dma_start(x[:, j, :], k.x[bass.ds(f * (P * TE) + j * P, P), :]).then_inc(x_in[j], 16)
                if moe:
                    if not isinstance(i, int) or i > 0:
                        eng.wait_ge(S.share_done, i)
                    eng.dma_start(rec[:, n, :, :], k.rec_d[:, bass.ds(i * RPP, RPP), :]).then_inc(rec_in[n], 16)
                    eng.dma_start(pos[:, n, :], k.pos_d[:, bass.ds(i * RPP, RPP)]).then_inc(rec_in[n], 16)
                if back:
                    for j in range(TE):
                        rows = bass.ds(b * (P * TE) + j * P, P)
                        eng.wait_ge(S.y_ready, b * TE + j + 1)
                        eng.dma_start(k.x2[rows, :], acc[:, 1 - n, j, :]).then_inc(out_done[j], 16)
                        eng.dma_start(k.table1[rows, :], y[:, j, 0:D]).then_inc(out_done[j], 16)

            pipeline(eng, run)
            for j in range(TE):
                eng.wait_ge(out_done[j], 32 * (NP + 1))

        @block.gpsimd
        def _(eng):
            eng.memset(neg_half[:], -0.5).then_inc(S.power_ready, 1)
            eng.wait_ge(S.power_ready, 1)
            eng.sem_inc(S.share_done, 1)

            def rstd(which, pair):
                eng.wait_ge(mv_ready[which], pair + 1)
                eng.nop(nofuse=True)
                eng.tensor_scalar(ve[:, which, :], mv[:, which, :, 1], LN_EPS, None, ALU.add).then_inc(rs_steps[which], 1)
                eng.wait_ge(rs_steps[which], pair + 1)
                eng.nop(nofuse=True)
                eng.tensor_tensor(rs[:, which, :], ve[:, which, :], neg_half[:], ALU.pow).then_inc(rs_ready[which], 1)

            def run(i, n, turn, front=True, moe=True, back=True):
                f, b = (i + 1 if moe else i), i - 1

                shares = [0, RPP // 4, RPP * 5 // 12, RPP // 2, RPP]

                def scatter(part):
                    if not moe:
                        return
                    if part == 0:
                        eng.wait_ge(rec_in[n], turn * 32 + 32)
                        eng.nop(nofuse=True)
                    for r in range(shares[part], shares[part + 1]):
                        eng.indirect_dma_start(
                            out=k.sorted_recs, out_offset=bass.IndirectOffsetOnAxis(ap=pos[:, n, r:r + 1], axis=0),
                            in_=rec[:, n, r, :], in_offset=None).then_inc(scattered[n], 16)

                if back:
                    rstd(LN_X2, b)
                scatter(0)
                if front:
                    rstd(LN_H, f)
                scatter(1)
                if front:
                    rstd(LN_MIX, f)
                scatter(2)
                if front:
                    rstd(LN_X1, f)
                scatter(3)
                if moe and (not isinstance(i, int) or i > 0):
                    eng.wait_ge(scattered[1 - n], (turn + n) * (16 * RPP))
                    eng.sem_inc(S.share_done, 1)

            pipeline(eng, run)
            for n in range(2):
                eng.wait_ge(scattered[n], 16 * RPP * (NP // 2))
                eng.nop(nofuse=True)

        @block.vector
        def _(eng):
            eng.wait_ge(w_in, 8 * 16)
            eng.tensor_scalar(half_gamma[:], half_gamma[:], 0.5, None, ALU.mult).then_inc(S.consts, 1)
            eng.tensor_scalar(half_beta[:], half_beta[:], 0.5, None, ALU.mult).then_inc(S.consts, 1)
            eng.memset(ones[:], 1.0).then_inc(S.setup, 1)
            eng.memset(zeros[:], 0.0).then_inc(S.setup, 1)
            eng.memset(y[:, :, D:D + 1], 1.0).then_inc(S.setup, 1)
            eng.wait_ge(S.setup_mm, 1)
            eng.tensor_copy(b1[:, :, :], ps_T[:, 0:2, 0:NE]).then_inc(S.setup, 1)
            eng.tensor_copy(w_r[:, :, :], ps_T[:, 2:4, 0:NE]).then_inc(S.setup, 1)
            eng.wait_ge(S.consts, 2)
            eng.sem_inc(S.dn_kept, 2)

            def heads(ap):
                return ap.rearrange("p (h c) -> p h c", c=32)

            def spread(ap):
                return ap.unsqueeze(2).to_broadcast([P, 8, 32])

            def statistics(which, pair, tiles, sem_, value):
                for j in range(TE):
                    eng.wait_ge(sem_, value(j))
                    eng.bn_stats(st[:, which, j, :], tiles[:, j, :]).then_inc(st_done[which], 1)
                eng.wait_ge(st_done[which], pair * TE + TE)
                eng.nop(nofuse=True)
                for j in range(TE):
                    ins = eng.bn_aggr(mv[:, which, j, :], st[:, which, j, :])
                ins.then_inc(mv_ready[which], 1)

            def run(i, n, turn, front=True, moe=True, back=True):
                f, b = (i + 1 if moe else i), i - 1
                fn = 1 - n if moe else n

                def expert_sum(e, j):
                    at = i * 16 + e * 2 + j
                    eng.wait_ge(S.dn_done, at + 1)
                    if e == 0:
                        eng.wait_ge(S.acc_ready, i * TE + j + 1)
                    else:
                        eng.wait_ge(S.dn_kept, at + 1)
                    eng.scalar_tensor_tensor(out=acc[:, n, j, :], in0=ps_dn[j][:, :], scalar=comb[:, n, j, e:e + 1],
                                             in1=acc[:, n, j, :], op0=ALU.mult, op1=ALU.add).then_inc(S.dn_kept, 1)

                def add_b2(j):
                    eng.wait_ge(S.b2_done, i * TE + j + 1)
                    eng.wait_ge(S.xt_added, i * TE + j + 1)
                    eng.tensor_tensor(acc[:, n, j, :], acc[:, n, j, :], ps_M[:, :], ALU.add).then_inc(S.acc_ready, 1)

                def back_norm():
                    statistics(LN_X2, b, acc[:, 1 - n, :, :], S.dn_kept, lambda j: b * 16 + 2 + 15 + j)

                def back_rows():
                    eng.wait_ge(rs_ready[LN_X2], b + 1)
                    for j in range(TE):
                        t = b * TE + j
                        eng.wait_ge(out_done[j], b * 32 + 32)
                        eng.wait_ge(S.ctx_done, t + 1)
                        eng.tensor_scalar(y[:, j, 0:D], acc[:, 1 - n, j, :], mv[:, LN_X2, j, 0:1],
                                          rs[:, LN_X2, j:j + 1], ALU.subtract, ALU.mult).then_inc(S.y_ready, 1)

                def back_phi(j):
                    eng.wait_ge(S.k_exp, b * TE + j + 1)
                    eng.tensor_tensor(krelu[:, j, :], kexp[:, j, :], krelu[:, j, :], ALU.add).then_inc(S.phi_ready, 1)

                def x_and_sums(j):
                    t = f * TE + j
                    eng.wait_ge(x_in[j], f * 16 + 16)
                    if moe:
                        eng.wait_ge(S.h_chain, f * 10 - 1 + j)
                        eng.wait_ge(S.T_done, t - 1)
                    eng.tensor_scalar(xn[:, j, :], x[:, j, :], k.mean[:, bass.ds(t, 1)], k.rstd[:, bass.ds(t, 1)],
                                      ALU.subtract, ALU.mult).then_inc(S.xs_ready, 1)
                    eng.wait_ge(S.xs_ready, t * 2 + 1)
                    eng.scalar_tensor_tensor(out=s[:, j, :], in0=xn[:, j, :], scalar=k.dinv[:, bass.ds(t, 1)],
                                             in1=k.sums[:, bass.ds(t, 1), :].rearrange("p a d -> p (a d)"),
                                             op0=ALU.mult, op1=ALU.add).then_inc(S.xs_ready, 1)

                def gcn(j):
                    t = f * TE + j
                    eng.wait_ge(S.h_done, t + 1)
                    eng.scalar_tensor_tensor(out=h[:, j, :], in0=ps_M[:, :], scalar=k.dinv[:, bass.ds(t, 1)],
                                             in1=b_gcn[:], op0=ALU.mult, op1=ALU.add).then_inc(S.h_kept, 1)

                def query(j):
                    t = f * TE + j
                    eng.wait_ge(S.q_done, t + 1)
                    eng.tensor_reduce(qmax[:, j, :], heads(ps_M[:, :]), AX.X, ALU.max).then_inc(S.q_chain, 1)
                    eng.wait_ge(S.q_chain, f * 6 + j + 1)
                    if moe:
                        eng.wait_ge(S.qT_done, t - 1)
                    eng.tensor_tensor(heads(q[:, j, :]), heads(ps_M[:, :]), spread(qmax[:, j, :]), ALU.subtract)\
                       .then_inc(S.q_kept, 1)

                def query_softmax(j):
                    t = f * TE + j
                    eng.wait_ge(S.q_exp, t + 1)
                    eng.tensor_reduce(qsum[:, j, :], heads(q[:, j, :]), AX.X, ALU.add).then_inc(S.q_chain, 1)
                    eng.wait_ge(S.q_chain, f * 6 + 3 + 2 * j)
                    eng.reciprocal(qrec[:, j, :], qsum[:, j, :]).then_inc(S.q_chain, 1)
                    eng.wait_ge(S.q_chain, f * 6 + 4 + 2 * j)
                    eng.tensor_tensor(heads(q[:, j, :]), heads(q[:, j, :]), spread(qrec[:, j, :]), ALU.mult)\
                       .then_inc(S.qn_ready, 1)

                def gcn_residual():
                    eng.wait_ge(rs_ready[LN_H], f + 1)
                    for step in range(5):
                        for j in range(TE):
                            if step:
                                eng.wait_ge(S.h_chain, f * 10 + step * 2 - 1 + j)
                            hj = h[:, j, :]
                            if step == 0:
                                ins = eng.tensor_scalar(hj, hj, mv[:, LN_H, j, 0:1], rs[:, LN_H, j:j + 1],
                                                        ALU.subtract, ALU.mult)
                            elif step == 1:
                                ins = eng.tensor_tensor(hj, hj, half_gamma[:], ALU.mult)
                            elif step == 2:
                                ins = eng.tensor_tensor(hj, hj, half_beta[:], ALU.add)
                            elif step == 3:
                                ins = eng.scalar_tensor_tensor(out=hj, in0=xn[:, j, :], scalar=0.5, in1=hj,
                                                               op0=ALU.mult, op1=ALU.add)
                            else:
                                if moe:
                                    eng.wait_ge(out_done[j], f * 32)
                                ins = eng.scalar_tensor_tensor(out=acc[:, fn, j, :], in0=hj, scalar=0.0,
                                                               in1=x[:, j, :], op0=ALU.max, op1=ALU.add)
                            ins.then_inc(S.h_chain, 1)

                def mixer_residual():
                    eng.wait_ge(rs_ready[LN_MIX], f + 1)
                    for step in range(3):
                        for j in range(TE):
                            if step:
                                eng.wait_ge(S.m_chain, f * 6 + step * 2 - 1 + j)
                            mj = mix[:, j, :]
                            if step == 0:
                                ins = eng.tensor_scalar(mj, mj, mv[:, LN_MIX, j, 0:1], rs[:, LN_MIX, j:j + 1],
                                                        ALU.subtract, ALU.mult)
                            elif step == 1:
                                ins = eng.tensor_tensor(mj, mj, mix_gamma[:], ALU.mult)
                            else:
                                ins = eng.tensor_tensor(acc[:, fn, j, :], acc[:, fn, j, :], mj, ALU.add)
                            ins.then_inc(S.m_chain, 1)
                    statistics(LN_X1, f, acc[:, fn, :, :], S.m_chain, lambda j: f * 6 + 5 + j)

                def tokens():
                    eng.wait_ge(rs_ready[LN_X1], f + 1)
                    for j in range(TE):
                        if moe:
                            eng.wait_ge(S.xt_added, f * TE + j - 1)
                        eng.tensor_scalar(xt[:, j, :], acc[:, fn, j, :], mv[:, LN_X1, j, 0:1], rs[:, LN_X1, j:j + 1],
                                          ALU.subtract, ALU.mult).then_inc(S.xt_ready, 1)
                    for j in range(TE):
                        eng.wait_ge(S.xt_ready, f * TE + j + 1)
                        eng.tensor_tensor(acc[:, fn, j, :], acc[:, fn, j, :], xt[:, j, :], ALU.add)\
                           .then_inc(S.xt_added, 1)

                def router(steps):
                    for step in steps:
                        for j in range(TE):
                            t = f * TE + j
                            lj, ej, tj = logit[:, j, :], expl[:, j, :], top[:, j, :]
                            if step == 0:
                                eng.wait_ge(S.r_done, t + 1)
                                eng.tensor_copy(lj, ps_M[:, 0:NE]).then_inc(S.r_kept, 1)
                                continue
                            if step == 1:
                                eng.wait_ge(S.r_kept, t + 1)
                                eng.nop(nofuse=True)
                                ins = eng.max(tj, lj)
                            else:
                                eng.wait_ge(S.r_chain, f * 28 + (step - 1) * 2 - 1 + j)
                            if step == 3:
                                eng.wait_ge(S.r_exp, t + 1)
                            if step == 2:
                                ins = eng.tensor_scalar(gate[:, j, 0:1], tj[:, 0:1], -1.0, None, ALU.mult)
                            elif step == 3:
                                ins = eng.tensor_reduce(gate[:, j, 1:2], ej, AX.X, ALU.add)
                            elif step == 4:
                                ins = eng.reciprocal(gate[:, j, 2:3], gate[:, j, 1:2])
                            elif step == 5:
                                ins = eng.tensor_scalar(ej, ej, gate[:, j, 2:3], None, ALU.mult)
                            elif step == 6:
                                eng.nop(nofuse=True)
                                ins = eng.max(tj, ej)
                            elif step == 7:
                                eng.nop(nofuse=True)
                                ins = eng.max_index(top_i[:, j, :], tj, ej)
                            elif step == 8:
                                ins = eng.tensor_copy(top_f[:, j, :], top_i[:, j, 0:2])
                            elif step == 9:
                                ins = eng.tensor_tensor(gate[:, j, 3:4], tj[:, 0:1], tj[:, 1:2], ALU.add)
                            elif step == 10:
                                ins = eng.tensor_scalar(gate[:, j, 3:4], gate[:, j, 3:4], 1e-12, None, ALU.max)
                            elif step == 11:
                                ins = eng.reciprocal(gate[:, j, 3:4], gate[:, j, 3:4])
                            elif step == 12:
                                ins = eng.tensor_scalar(tj[:, 0:2], tj[:, 0:2], gate[:, j, 3:4], None, ALU.mult)
                            elif step == 13:
                                ins = eng.tensor_scalar(pick[:, j, 0, :], k.lane[0:P, 0:NE], top_f[:, j, 0:1],
                                                        tj[:, 0:1], ALU.is_equal, ALU.mult)
                            elif step == 14:
                                ins = eng.tensor_scalar(pick[:, j, 1, :], k.lane[0:P, 0:NE], top_f[:, j, 1:2],
                                                        tj[:, 1:2], ALU.is_equal, ALU.mult)
                            elif step == 15:
                                eng.wait_ge(S.r_chain, f * 28 + 28)
                                eng.tensor_tensor(comb[:, fn, j, :], pick[:, j, 0, :], pick[:, j, 1, :], ALU.add)\
                                   .then_inc(S.comb_ready, 1)
                                continue
                            ins.then_inc(S.r_chain, 1)

                for slot in range(32):
                    if moe:
                        if slot == 1 or slot == 2:
                            add_b2(slot - 1)
                        kind, e, c = chunk(slot)
                        if kind == "down":
                            expert_sum(e, c)
                    if back:
                        if slot == 0:
                            back_norm()
                        elif slot == 3:
                            back_rows()
                        elif slot == 12:
                            back_phi(0)
                            back_phi(1)
                    if front:
                        if slot < 2:
                            x_and_sums(slot)
                        elif slot == 4 or slot == 6:
                            gcn(slot // 2 - 2)
                            if slot == 6:
                                statistics(LN_H, f, h[:, :, :], S.h_kept, lambda j: f * TE + j + 1)
                        elif slot == 5 or slot == 7:
                            query((slot - 5) // 2)
                        elif slot == 8 or slot == 9:
                            query_softmax(slot - 8)
                        elif slot == 13:
                            gcn_residual()
                        elif slot == 17:
                            statistics(LN_MIX, f, mix[:, :, :], S.mix_kept, lambda j: f * TE + j + 1)
                        elif slot == 20:
                            mixer_residual()
                        elif slot == 23:
                            tokens()
                        elif slot == 27:
                            router(range(0, 3))
                        elif slot == 28:
                            router(range(3, 16))

            pipeline(eng, run)
            eng.wait_ge(S.ctx_done, 2 + k.NT)
            for c in range(2):
                eng.tensor_copy(k.context[:, c, :], ps_ctx[c][:, :])

        @block.scalar
        def _(eng):
            eng.sem_inc(S.up_kept, 2)

            def run(i, n, turn, front=True, moe=True, back=True):
                f, b = (i + 1 if moe else i), i - 1
                fn = 1 - n if moe else n
                inner = not isinstance(i, int)

                def gelu(e, c):
                    at = i * 16 + e * 2
                    eng.wait_ge(S.up_done, at + c + 1)
                    if inner or i > 0 or e >= 2:
                        eng.wait_ge(S.dn_done, at - 2)
                    eng.activation(hid[:, e % 2, c, :], ps_up[c][:, :], ACT.Gelu, bias=b1[:, c, e:e + 1])\
                       .then_inc(S.up_kept, 1)

                def keep_turned(j):
                    t = f * TE + j
                    eng.wait_ge(S.T_done, t + 1)
                    if moe:
                        eng.wait_ge(S.q_done, t - 1)
                    eng.copy(xsT[:, j, :, :], ps_T[:, :, :]).then_inc(S.T_kept, 1)

                def exp_query(j):
                    eng.wait_ge(S.q_kept, f * TE + j + 1)
                    eng.activation(q[:, j, :], q[:, j, :], ACT.Exp).then_inc(S.q_exp, 1)

                def keep_y(j):
                    t = b * TE + j
                    eng.wait_ge(S.yT_done, t + 1)
                    eng.wait_ge(S.k_done, t + 1)
                    eng.copy(yT[:, j, :, :], ps_T[:, 0:2, :]).then_inc(S.yT_kept, 1)

                def keys(j):
                    t = b * TE + j
                    eng.wait_ge(S.k_done, t + 3)
                    eng.wait_ge(S.ctx_done, t + 1)
                    eng.activation(kexp[:, j, :], ps_M[:, :], ACT.Relu, scale=-1.0).then_inc(S.k_below, 1)
                    eng.activation(krelu[:, j, :], ps_M[:, :], ACT.Relu).then_inc(S.k_kept, 1)

                def exp_key(j):
                    t = b * TE + j
                    eng.wait_ge(S.k_below, t + 1)
                    eng.activation(kexp[:, j, :], kexp[:, j, :], ACT.Exp, scale=-1.0).then_inc(S.k_exp, 1)

                def keep_query(j):
                    t = f * TE + j
                    eng.wait_ge(S.qT_done, t + 1)
                    if moe:
                        eng.wait_ge(S.mix_done, t - 1)
                    eng.copy(qT[:, j, :, :], ps_T[:, 0:2, :]).then_inc(S.qT_kept, 1)

                def keep_mix(j):
                    t = f * TE + j
                    eng.wait_ge(S.mix_done, t + 1)
                    if moe:
                        eng.wait_ge(S.m_chain, f * 6)
                    eng.copy(mix[:, j, :], ps_M[:, :]).then_inc(S.mix_kept, 1)

                def keep_tokens(j):
                    t = f * TE + j
                    eng.wait_ge(S.xT_done, t + 1)
                    if inner:
                        eng.wait_ge(S.up_done, f * 16 - 16)
                    eng.copy(xtT[:, fn, :, j, :], ps_T[:, 0:2, :]).then_inc(S.xT_kept, 1)

                def exp_router(j):
                    t = f * TE + j
                    eng.wait_ge(S.r_chain, f * 28 + 3 + j)
                    eng.activation(expl[:, j, :], logit[:, j, :], ACT.Exp, bias=gate[:, j, 0:1]).then_inc(S.r_exp, 1)

                def keep_gates(j):
                    t = f * TE + j
                    eng.wait_ge(S.cT_done, t + 1)
                    if moe:
                        eng.wait_ge(S.b2_done, t - 1)
                    eng.copy(combT[:, j, :], ps_T[0:NE, 0, :]).then_inc(S.cT_kept, 1)

                for slot in range(32):
                    if moe:
                        kind, e, c = chunk(slot)
                        if kind == "up":
                            gelu(e, c)
                    if front:
                        if slot == 2 or slot == 3:
                            keep_turned(slot - 2)
                        elif slot == 7:
                            exp_query(0)
                            exp_query(1)
                    if back:
                        if slot == 8 or slot == 9:
                            keep_y(slot - 8)
                        elif slot == 10 or slot == 11:
                            keys(slot - 10)
                        if slot == 11:
                            exp_key(0)
                            exp_key(1)
                    if front:
                        if slot == 13 or slot == 14:
                            keep_query(slot - 13)
                        elif slot == 15 or slot == 16:
                            keep_mix(slot - 15)
                        elif slot == 24 or slot == 25:
                            keep_tokens(slot - 24)
                        elif slot == 27:
                            exp_router(0)
                            exp_router(1)
                        elif slot == 30 or slot == 31:
                            keep_gates(slot - 30)

            pipeline(eng, run)

        @block.tensor
        def _(eng):
            eng.sem_inc(S.k_done, 2)
            eng.sem_inc(S.ctx_done, 2)
            eng.wait_ge(w_in, 8 * 16)
            for c in range(2):
                eng.transpose(ps_T[:, c, 0:NE], b1_raw[:, c * H2:(c + 1) * H2], k.ident[0:NE, 0:NE])
                mm = eng.transpose(ps_T[:, 2 + c, 0:NE], w_r_raw[:, c * H2:(c + 1) * H2], k.ident[0:NE, 0:NE])
            mm.then_inc(S.setup_mm, 1)
            eng.wait_ge(S.setup, 5)
            for c in range(2):
                eng.matmul(ps_ctx[c][:, :], zeros[:, 0:128], zeros[:, :], start=True, stop=False, skip_group_check=True)
            eng.wait_ge(e_in, 16 * 15)
            eng.wait_ge(out_done[0], 32)
            eng.wait_ge(out_done[1], 32)

            def run(i, n, turn, front=True, moe=True, back=True):
                f, b = (i + 1 if moe else i), i - 1
                fn = 1 - n if moe else n

                def up(e, c):
                    at = i * 16 + e * 2 + c
                    if e == 0:
                        eng.wait_ge(S.xT_kept, i * TE + TE)
                    eng.wait_ge(S.up_kept, at + 1)
                    for m in range(2):
                        mm = eng.matmul(ps_up[c][:, :], w1[:, e, m, c * H2:(c + 1) * H2], xtT[:, n, m, :, :],
                                        start=(m == 0), stop=(m == 1))
                    mm.then_inc(S.up_done, 1)

                def down(e, j):
                    eng.wait_ge(S.up_kept, i * 16 + e * 2 + 4)
                    eng.wait_ge(S.dn_kept, i * 16 + e * 2 + j + 1)
                    for m in range(2):
                        mm = eng.matmul(ps_dn[j][:, :], hid[:, e % 2, m, j * P:(j + 1) * P], w2[:, e, m, :],
                                        start=(m == 0), stop=(m == 1))
                    mm.then_inc(S.dn_done, 1)

                def second_bias(j):
                    if j == 0:
                        eng.wait_ge(S.r_kept, i * TE + TE)
                    else:
                        eng.wait_ge(S.acc_ready, i * TE + 1)
                    eng.wait_ge(S.cT_kept, i * TE + j + 1)
                    eng.matmul(ps_M[:, :], combT[:, j, :], b2[:], start=True, stop=True).then_inc(S.b2_done, 1)

                def turn_xs(j):
                    if j == 0 and moe:
                        eng.wait_ge(S.cT_kept, i * TE + TE)
                    if j == 1:
                        eng.wait_ge(S.T_kept, f * TE + 1)
                    eng.wait_ge(S.xs_ready, (f * TE + j) * 2 + 2)
                    for c in range(2):
                        eng.transpose(ps_T[:, c, :], xn[:, j, c * H2:(c + 1) * H2], k.ident[0:P, 0:P])
                        mm = eng.transpose(ps_T[:, 2 + c, :], s[:, j, c * H2:(c + 1) * H2], k.ident[0:P, 0:P])
                    mm.then_inc(S.T_done, 1)

                def product(lhs, rhs, bias=None):
                    for m in range(2):
                        mm = eng.matmul(ps_M[:, 0:rhs.shape[-1]], lhs[m], rhs[:, m, :], start=(m == 0),
                                        stop=(m == 1 and bias is None))
                    if bias is not None:
                        mm = eng.matmul(ps_M[:, :], ones[:], bias[:], start=False, stop=True)
                    return mm

                def gcn(j):
                    if j == 0 and moe:
                        eng.wait_ge(S.acc_ready, i * TE + TE)
                    if j == 1:
                        eng.wait_ge(S.q_kept, f * TE + 1)
                    eng.wait_ge(S.T_kept, f * TE + j + 1)
                    product([xsT[:, j, 2, :], xsT[:, j, 3, :]], w_gcn).then_inc(S.h_done, 1)

                def query(j):
                    eng.wait_ge(S.h_kept, f * TE + j + 1)
                    product([xsT[:, j, 0, :], xsT[:, j, 1, :]], w_q).then_inc(S.q_done, 1)

                def turn(src, j):
                    for c in range(2):
                        mm = eng.transpose(ps_T[:, c, :], src[:, j, c * H2:(c + 1) * H2], k.ident[0:P, 0:P])
                    return mm

                def turn_y(j):
                    if j == 1:
                        eng.wait_ge(S.yT_kept, b * TE + 1)
                    elif front:
                        eng.wait_ge(S.T_kept, f * TE + TE)
                    elif moe:
                        eng.wait_ge(S.cT_kept, i * TE + TE)
                    else:
                        eng.wait_ge(S.yT_kept, b * TE)
                    eng.wait_ge(S.y_ready, b * TE + j + 1)
                    turn(y, j).then_inc(S.yT_done, 1)

                def keys(j):
                    if j == 1:
                        eng.wait_ge(S.k_kept, b * TE + 1)
                    elif front:
                        eng.wait_ge(S.q_kept, f * TE + TE)
                    elif moe:
                        eng.wait_ge(S.acc_ready, i * TE + TE)
                    else:
                        eng.wait_ge(S.k_kept, b * TE)
                    eng.wait_ge(S.yT_kept, b * TE + j + 1)
                    product([yT[:, j, 0, :], yT[:, j, 1, :]], w_k, bias=b_k).then_inc(S.k_done, 1)

                def turn_query(j):
                    if j == 1:
                        eng.wait_ge(S.qT_kept, f * TE + 1)
                    elif back:
                        eng.wait_ge(S.yT_kept, b * TE + TE)
                    else:
                        eng.wait_ge(S.T_kept, f * TE + TE)
                    eng.wait_ge(S.qn_ready, f * TE + j + 1)
                    turn(q, j).then_inc(S.qT_done, 1)

                def mixer(j):
                    if j == 1:
                        eng.wait_ge(S.mix_kept, f * TE + 1)
                    elif back:
                        eng.wait_ge(S.k_kept, b * TE + TE)
                    else:
                        eng.wait_ge(S.q_kept, f * TE + TE)
                    eng.wait_ge(S.qT_kept, f * TE + j + 1)
                    product([qT[:, j, 0, :], qT[:, j, 1, :]], k.composed).then_inc(S.mix_done, 1)

                def context(j):
                    eng.wait_ge(S.phi_ready, b * TE + j + 1)
                    for c in range(2):
                        mm = eng.matmul(ps_ctx[c][:, :], krelu[:, j, c * H2:(c + 1) * H2], y[:, j, :],
                                        start=False, stop=False, skip_group_check=True)
                    mm.then_inc(S.ctx_done, 1)

                def turn_tokens(j):
                    eng.wait_ge(S.xT_kept if j else S.qT_kept, f * TE + (1 if j else TE))
                    eng.wait_ge(S.xt_ready, f * TE + j + 1)
                    turn(xt, j).then_inc(S.xT_done, 1)

                def router(j):
                    eng.wait_ge(S.r_kept if j else S.mix_kept, f * TE + (1 if j else TE))
                    eng.wait_ge(S.xT_kept, f * TE + j + 1)
                    product([xtT[:, fn, 0, j, :], xtT[:, fn, 1, j, :]], w_r).then_inc(S.r_done, 1)

                def turn_gates(j):
                    eng.wait_ge(S.cT_kept if j else S.xT_kept, f * TE + (1 if j else TE))
                    eng.wait_ge(S.comb_ready, f * TE + j + 1)
                    eng.transpose(ps_T[0:NE, 0, :], comb[:, fn, j, :], k.ident[0:P, 0:P]).then_inc(S.cT_done, 1)

                for slot in range(32):
                    if moe:
                        if slot < 2:
                            second_bias(slot)
                        kind, e, c = chunk(slot)
                        (up if kind == "up" else down)(e, c)
                    if front:
                        if slot == 2 or slot == 3:
                            turn_xs(slot - 2)
                        elif slot == 4 or slot == 6:
                            gcn(slot // 2 - 2)
                        elif slot == 5 or slot == 7:
                            query((slot - 5) // 2)
                    if back:
                        if slot == 8 or slot == 9:
                            turn_y(slot - 8)
                        elif slot == 10 or slot == 11:
                            keys(slot - 10)
                        elif slot == 17 or slot == 18:
                            context(slot - 17)
                    if front:
                        if slot == 13 or slot == 14:
                            turn_query(slot - 13)
                        elif slot == 15 or slot == 16:
                            mixer(slot - 15)
                        elif slot == 24 or slot == 25:
                            turn_tokens(slot - 24)
                        elif slot == 26 or slot == 27:
                            router(slot - 26)
                        elif slot == 30 or slot == 31:
                            turn_gates(slot - 30)

            pipeline(eng, run)


def sum_layer1(nc, k):
    NF = k.L1_mix_W1.shape[1] // 128
    T = TS * P
    with ExitStack() as ctx:
        sb, pb, sem = allocators(nc, ctx, "sum1")
        agg = Aggregation(nc, k, sb, pb, sem, k.table1)
        wq = sb("wq", [128, 2, D])
        w1 = sb("w1", [128, 2, NF * 128])
        w2 = sb("w2", [128, NF, D])
        bq = sb("bq", [128, 2])
        neg_bq = sb("neg_bq", [128, 2])
        b1 = sb("b1", [128, NF])
        bo = sb("bo", [1, D])
        b2 = sb("b2", [1, D])
        ones = sb("ones", [1, P])
        gamma = [sb(f"gamma{n}", [P, D]) for n in range(2)]
        beta = [sb(f"beta{n}", [P, D]) for n in range(2)]
        neg_half = sb("neg_half", [P, TS])
        xn = sb("xn", [P, TS, D])
        y = sb("y", [P, TS, D])
        xT = sb("x_T", [128, 2, T])
        phi = sb("phi", [128, 2, T])
        low = sb("low", [128, 2, T])
        hid = low
        st = sb("stats", [P, TS, 6])
        mv = sb("mean_var", [P, 2, TS, 2])
        ve = sb("var_eps", [P, 2, TS])
        rs = sb("rstds", [P, 2, TS])
        ps_A = [pb(f"ps_A{n}", [128, 512]) for n in range(2)]
        ps_C = [pb(f"ps_C{n}", [128, 512]) for n in range(2)]

        w_in, x_in, stored = (sem(n) for n in ("w_in", "x_in", "stored"))
        names = ("consts", "power_ready", "T1_done", "T1_kept", "q_done", "q_below", "q_kept", "q_exp", "phi_ready",
                 "den_done", "z_chain", "phin_ready", "attn_done", "y_added", "y1_steps", "y1_ready", "T2_done",
                 "T2_kept", "up_done", "up_kept", "dn_done", "ff_added", "y2_steps", "y2_ready")
        S = Shared()
        (S.consts, S.power_ready, S.T1_done, S.T1_kept, S.q_done, S.q_below, S.q_kept, S.q_exp, S.phi_ready,
         S.den_done, S.z_chain, S.phin_ready, S.attn_done, S.y_added, S.y1_steps, S.y1_ready, S.T2_done, S.T2_kept,
         S.up_done, S.up_kept, S.dn_done, S.ff_added, S.y2_steps, S.y2_ready) = (sem(n) for n in names)
        st_done, mv_ready, rs_steps, rs_ready = ([sem(f"{name}{w}") for w in range(2)]
                                                 for name in ("st_done", "mv_ready", "rs_steps", "rs_ready"))
        block = ctx.enter_context(nc.Block())

        def supertiles(eng, run):
            run(0)
            with eng.Fori(1, k.NSUP) as i:
                run(i)

        def after(eng, sem_, count):
            if not isinstance(count, int) or count > 0:
                eng.wait_ge(sem_, count)

        def rows_of(i):
            return bass.ds(i * T, T)

        @block.sync
        def _(eng):
            def row(ap, n):
                return ap.rearrange("(a n) -> a n", a=1).to_broadcast([n, D])

            def weights():
                yield wq[:, :, :], k.L1_mix_Wq.rearrange("(c p) n -> p c n", c=2)
                yield w1[:, :, :], k.L1_mix_W1.rearrange("(c p) n -> p c n", c=2)
                yield w2[:, :, :], k.L1_mix_W2.rearrange("(c p) n -> p c n", c=NF)
                yield bq[:, :], k.L1_mix_bq.rearrange("(c p) -> p c", c=2)
                yield b1[:, :], k.L1_mix_b1.rearrange("(c p) -> p c", c=NF)
                yield bo[:], k.L1_mix_bo.rearrange("(a n) -> a n", a=1)
                yield b2[:], k.L1_mix_b2.rearrange("(a n) -> a n", a=1)
                yield gamma[0][:], row(k.L1_mix_ln1_g, P)
                yield beta[0][:], row(k.L1_mix_ln1_b, P)
                yield gamma[1][:], row(k.L1_mix_ln2_g, P)
                yield beta[1][:], row(k.L1_mix_ln2_b, P)

            for out, in_ in weights():
                eng.dma_start(out, in_, allow_slow_non_contiguous=True).then_inc(w_in, 16)

            def load(i):
                after(eng, S.y_added, i * 2)
                eng.dma_start(xn[:, :, :], k.table1[rows_of(i), :].rearrange("(t p) d -> p t d", p=P)).then_inc(x_in, 16)

            def store(i):
                eng.wait_ge(S.y2_ready, i + 1)
                eng.dma_start(k.mixed[rows_of(i), :].rearrange("(t p) d -> p t d", p=P), y[:, :, :]).then_inc(stored, 16)

            load(0)
            with eng.Fori(1, k.NSUP) as i:
                load(i)
                store(i - 1)
            store(k.NSUP - 1)
            eng.wait_ge(stored, 16 * k.NSUP)

        @block.gpsimd
        def _(eng):
            eng.memset(neg_half[:], -0.5).then_inc(S.power_ready, 1)
            eng.wait_ge(S.power_ready, 1)

            def rstd(which, i):
                eng.wait_ge(mv_ready[which], i + 1)
                eng.nop(nofuse=True)
                eng.tensor_scalar(ve[:, which, :], mv[:, which, :, 1], LN_EPS, None, ALU.add).then_inc(rs_steps[which], 1)
                eng.wait_ge(rs_steps[which], i + 1)
                eng.nop(nofuse=True)
                eng.tensor_tensor(rs[:, which, :], ve[:, which, :], neg_half[:], ALU.pow).then_inc(rs_ready[which], 1)

            def run(i):
                first = isinstance(i, int)
                for half in range(2):
                    agg.take_indices(i, half)
                    for g in range(half * GRPS // 2, (half + 1) * GRPS // 2):
                        if g == 3 and not first:
                            rstd(1, i - 1)
                        if g == 7:
                            rstd(0, i)
                        agg.gather_group(i, half, g)

            supertiles(eng, run)
            rstd(1, k.NSUP - 1)

        @block.vector
        def _(eng):
            agg.vector_start()
            eng.wait_ge(w_in, 11 * 16)
            eng.tensor_scalar(neg_bq[:], bq[:], -1.0, None, ALU.mult).then_inc(S.consts, 1)
            eng.memset(ones[:], 1.0).then_inc(S.consts, 1)

            def statistics(which, i):
                eng.wait_ge(st_done[which], i * TS + TS)
                eng.nop(nofuse=True)
                for j in range(TS):
                    ins = eng.bn_aggr(mv[:, which, j, :], st[:, j, :])
                ins.then_inc(mv_ready[which], 1)

            def normalise(which, i, steps, ready, part):
                if part == 0:
                    eng.wait_ge(rs_ready[which], i + 1)
                    for j in range(TS):
                        eng.tensor_scalar(y[:, j, :], y[:, j, :], mv[:, which, j, 0:1], rs[:, which, j:j + 1],
                                          ALU.subtract, ALU.mult).then_inc(steps, 1)
                elif part == 1:
                    eng.wait_ge(steps, i * 5 + 4)
                    eng.tensor_tensor(y[:, :, :], y[:, :, :], gamma[which][:].unsqueeze(1).to_broadcast([P, TS, D]),
                                      ALU.mult).then_inc(steps, 1)
                else:
                    eng.wait_ge(steps, i * 5 + 5)
                    eng.tensor_tensor(y[:, :, :], y[:, :, :], beta[which][:].unsqueeze(1).to_broadcast([P, TS, D]),
                                      ALU.add).then_inc(ready, 1)

            def add_phi(i, c):
                eng.wait_ge(S.q_exp, i * 2 + c + 1)
                eng.tensor_tensor(phi[:, c, :], phi[:, c, :], low[:, c, :], ALU.add).then_inc(S.phi_ready, 1)

            def divide(i, c):
                eng.wait_ge(S.den_done, i * 2 + c + 1)
                eng.wait_ge(S.phi_ready, i * 2 + c + 1)
                eng.tensor_scalar(low[:, c, :], ps_A[c][:, 0:T], 1e-6, None, ALU.add).then_inc(S.z_chain, 1)
                eng.wait_ge(S.z_chain, i * 4 + c * 2 + 1)
                eng.reciprocal(low[:, c, :], low[:, c, :]).then_inc(S.z_chain, 1)
                eng.wait_ge(S.z_chain, i * 4 + c * 2 + 2)
                eng.tensor_tensor(phi[:, c, :], phi[:, c, :], low[:, c, :], ALU.mult).then_inc(S.phin_ready, 1)

            def add_attention(i, n):
                eng.wait_ge(S.attn_done, i * 2 + n + 1)
                if n == 0:
                    after(eng, stored, i * 16)
                eng.tensor_tensor(y[:, 2 * n:2 * n + 2, :], ps_C[n][0:P, :].rearrange("p (t d) -> p t d", d=D),
                                  xn[:, 2 * n:2 * n + 2, :], ALU.add).then_inc(S.y_added, 1)
                eng.wait_ge(S.y_added, i * 2 + n + 1)
                if n == 0:
                    after(eng, mv_ready[1], i)
                for j in range(2 * n, 2 * n + 2):
                    eng.bn_stats(st[:, j, :], y[:, j, :]).then_inc(st_done[0], 1)
                if n == 1:
                    after(eng, rs_ready[0], i)
                    statistics(0, i)

            def add_feed_forward(i, n):
                eng.wait_ge(S.dn_done, (i + 1) * (NF + 1))
                eng.tensor_tensor(y[:, 2 * n:2 * n + 2, :], ps_A[n][0:P, :].rearrange("p (t d) -> p t d", d=D),
                                  y[:, 2 * n:2 * n + 2, :], ALU.add).then_inc(S.ff_added, 1)
                eng.wait_ge(S.ff_added, i * 2 + n + 1)
                for j in range(2 * n, 2 * n + 2):
                    eng.bn_stats(st[:, j, :], y[:, j, :]).then_inc(st_done[1], 1)
                if n == 1:
                    after(eng, rs_ready[1], i)
                    statistics(1, i)

            agg.take_local(0, 0, first=True)
            for l in range(GRP):
                agg.build(0, 0, l)

            def run(i):
                agg.take_local(i, i + 1)
                for h in range(2 * GRPS):
                    for l in range(h % 2 * GRP // 2, (h % 2 + 1) * GRP // 2):
                        agg.build(i, h // 2 + 1, l)
                        agg.add(i, h // 2, l)
                    if 2 <= h < 5 and not isinstance(i, int):
                        normalise(1, i - 1, S.y2_steps, S.y2_ready, h - 2)
                    if h == 3 or h == 4:
                        add_phi(i, h - 3)
                    elif h == 5 or h == 6:
                        divide(i, h - 5)
                    elif h == 8 or h == 9:
                        add_attention(i, h - 8)
                    elif 11 <= h < 14:
                        normalise(0, i, S.y1_steps, S.y1_ready, h - 11)
                    elif h == 23:
                        add_feed_forward(i, 0)
                        add_feed_forward(i, 1)

            supertiles(eng, run)
            for part in range(3):
                normalise(1, k.NSUP - 1, S.y2_steps, S.y2_ready, part)

        @block.scalar
        def _(eng):
            eng.wait_ge(S.consts, 2)

            def run(i):
                for c in range(2):
                    eng.wait_ge(S.T1_done, i * 2 + c + 1)
                    after(eng, S.up_done, i * NF)
                    eng.copy(xT[:, c, :], ps_A[c][:, 0:T]).then_inc(S.T1_kept, 1)
                for c in range(2):
                    if c == 1:
                        eng.wait_ge(S.q_below, i * 2 + 1)
                        eng.activation(low[:, 0, :], low[:, 0, :], ACT.Exp, scale=-1.0).then_inc(S.q_exp, 1)
                    eng.wait_ge(S.q_done, i * 2 + c + 1)
                    after(eng, S.attn_done, i * 2)
                    after(eng, S.phin_ready, i * 2)
                    eng.activation(low[:, c, :], ps_C[c][:, 0:T], ACT.Relu, bias=neg_bq[:, c:c + 1], scale=-1.0)\
                       .then_inc(S.q_below, 1)
                    eng.activation(phi[:, c, :], ps_C[c][:, 0:T], ACT.Relu, bias=bq[:, c:c + 1]).then_inc(S.q_kept, 1)
                eng.wait_ge(S.q_below, i * 2 + 2)
                eng.activation(low[:, 1, :], low[:, 1, :], ACT.Exp, scale=-1.0).then_inc(S.q_exp, 1)
                for c in range(2):
                    eng.wait_ge(S.T2_done, i * 2 + c + 1)
                    eng.wait_ge(S.q_done, i * 2 + 2)
                    eng.copy(xT[:, c, :], ps_A[c][:, 0:T]).then_inc(S.T2_kept, 1)
                for u in range(NF):
                    eng.wait_ge(S.up_done, i * NF + u + 1)
                    after(eng, S.dn_done, i * (NF + 1) + u)
                    eng.activation(hid[:, u % 2, :], ps_C[u % 2][:, 0:T], ACT.Relu, bias=b1[:, u:u + 1])\
                       .then_inc(S.up_kept, 1)

            supertiles(eng, run)

        @block.tensor
        def _(eng):
            agg.tensor_start()
            eng.wait_ge(w_in, 11 * 16)
            eng.wait_ge(S.consts, 2)

            def turn(src, ready, count, done):
                eng.wait_ge(ready, count)
                for c in range(2):
                    for j in range(TS):
                        mm = eng.transpose(ps_A[c][:, j * P:(j + 1) * P], src[:, j, c * H2:(c + 1) * H2],
                                           k.ident[0:P, 0:P])
                    mm.then_inc(done, 1)

            def queries(i, c):
                if c == 0:
                    eng.wait_ge(S.T1_kept, i * 2 + 2)
                after(eng, S.up_kept, i * NF)
                for m in range(2):
                    mm = eng.matmul(ps_C[c][:, 0:T], wq[:, m, c * H2:(c + 1) * H2], xT[:, m, :],
                                    start=(m == 0), stop=(m == 1))
                mm.then_inc(S.q_done, 1)

            def denominators(i, c):
                eng.wait_ge(S.phi_ready, i * 2 + c + 1)
                eng.matmul(ps_A[c][:, 0:T], k.key_sum_of[:, c, :], phi[:, c, :], start=True, stop=True)\
                   .then_inc(S.den_done, 1)

            def attention(i, n):
                eng.wait_ge(S.q_kept, i * 2 + 2)
                eng.wait_ge(S.phin_ready, i * 2 + 2)
                eng.matmul(ps_C[n][0:P, :], ones[:], bo[:].unsqueeze(1).to_broadcast([1, 2, D]), start=True, stop=False,
                           skip_group_check=True)
                for j in range(2 * n, 2 * n + 2):
                    for c in range(2):
                        mm = eng.matmul(ps_C[n][0:P, (j % 2) * D:(j % 2 + 1) * D], phi[:, c, j * P:(j + 1) * P],
                                        k.composed[:, c, :], start=False, stop=False, skip_group_check=True)
                mm.then_inc(S.attn_done, 1)

            def up(i, u):
                if u == 0:
                    eng.wait_ge(S.T2_kept, i * 2 + 2)
                if u < 2:
                    eng.wait_ge(S.y_added, i * 2 + 2)
                else:
                    eng.wait_ge(S.up_kept, i * NF + u - 1)
                for m in range(2):
                    mm = eng.matmul(ps_C[u % 2][:, 0:T], w1[:, m, u * 128:(u + 1) * 128], xT[:, m, :],
                                    start=(m == 0), stop=(m == 1))
                mm.then_inc(S.up_done, 1)

            def down_bias(i):
                eng.wait_ge(S.T2_kept, i * 2 + 2)
                for n in range(2):
                    mm = eng.matmul(ps_A[n][0:P, :], ones[:], b2[:].unsqueeze(1).to_broadcast([1, 2, D]), start=True, stop=False,
                                    skip_group_check=True)
                mm.then_inc(S.dn_done, 1)

            def down(i, u):
                eng.wait_ge(S.up_kept, i * NF + u + 1)
                for j in range(TS):
                    mm = eng.matmul(ps_A[j // 2][0:P, (j % 2) * D:(j % 2 + 1) * D], hid[:, u % 2, j * P:(j + 1) * P],
                                    w2[:, u, :], start=False, stop=False, skip_group_check=True)
                mm.then_inc(S.dn_done, 1)

            def run(i):
                for h in range(2 * GRPS):
                    agg.multiply(i, h // 2, h % 2)
                    if h == 0:
                        after(eng, S.ff_added, i * 2)
                        turn(xn, x_in, i * 16 + 16, S.T1_done)
                    elif h == 1 or h == 2:
                        queries(i, h - 1)
                    elif h == 5 or h == 6:
                        denominators(i, h - 5)
                    elif h == 8 or h == 9:
                        attention(i, h - 8)
                    elif h == 14:
                        turn(y, S.y1_ready, i + 1, S.T2_done)
                        down_bias(i)
                    elif h >= 15:
                        if h - 15 < NF:
                            up(i, h - 15)
                        if h > 15:
                            down(i, h - 16)

            supertiles(eng, run)


def prepare_slices(nc, k):
    G = 64
    with ExitStack() as ctx:
        sb, pb, sem = allocators(nc, ctx, "prep")
        wg = sb("wg", [128, 2, D])
        wx = sb("wx", [128, 2, 2 * D])
        wxT = sb("wx_T", [128, 4, D])
        pair = sb("slice_pair", [128, 128])
        bx = sb("bx", [128, 4])
        bs = sb("b_slice", [1, 8, G])
        temp = sb("temp", [128, 8])
        row = sb("bias_row", [1, 8, G])
        ones = sb("ones", [1, P])
        ps_g = pb("ps_g", [128, 2, D])
        ps_x = [pb(f"ps_x{n}", [128, 2, D]) for n in range(2)]
        ps_c = [pb(f"ps_c{m}", [128, 8, G]) for m in range(2)]
        ps_b = pb("ps_b", [1, 8, G])
        ps_r = pb("ps_r", [P, 8 * G])
        cleared, w_in, ones_ready, turned, kept, comp_mm, chain, row_mm = (
            sem(n) for n in ("cleared", "w_in", "ones_ready", "turned", "kept", "comp_mm", "chain", "row_mm"))
        block = ctx.enter_context(nc.Block())

        @block.sync
        def _(eng):
            eng.dma_start(wg[:, :, :], k.L1_gnn_W.rearrange("(c p) n -> p c n", c=2)).then_inc(w_in, 16)
            eng.dma_start(wx[:, :, :], k.L1_ffn_W_x.rearrange("(c p) n -> p c n", c=2)).then_inc(w_in, 16)
            eng.dma_start(bx[:], k.L1_ffn_b_x.rearrange("(c p) -> p c", p=128), allow_slow_non_contiguous=True)\
               .then_inc(w_in, 16)
            eng.dma_start(bs[:, :, :], k.L1_ffn_b_slice.rearrange("(a b g) -> a b g", a=1, b=1).to_broadcast([1, 8, G]))\
               .then_inc(w_in, 16)
            eng.dma_start(temp[:], k.L1_ffn_temperature.rearrange("a h b c -> a (h b c)").to_broadcast([128, 8]))\
               .then_inc(w_in, 16)
            eng.dma_start(k.b_gnn2[:, 0, :], k.L1_gnn_bias.rearrange("(a n) -> a n", a=1)).then_inc(w_in, 16)
            eng.dma_start(k.b_gnn2[:, 1, :], k.L1_gnn_bias.rearrange("(a n) -> a n", a=1)).then_inc(w_in, 16)
            eng.wait_ge(cleared, 1)
            eng.nop(nofuse=True)
            eng.dma_start(pair[0:G, 0:G], k.L1_ffn_W_slice).then_inc(w_in, 16)
            eng.dma_start(pair[G:128, G:128], k.L1_ffn_W_slice).then_inc(w_in, 16)

        @block.gpsimd
        def _(eng):
            eng.memset(pair[:], 0.0).then_inc(cleared, 1)
            eng.memset(ones[:], 1.0).then_inc(ones_ready, 1)

        @block.vector
        def _(eng):
            eng.wait_ge(turned, 1)
            eng.tensor_copy(k.w_gnn[:, :, :], ps_g[:, :, :])
            for n in range(2):
                eng.wait_ge(turned, n + 2)
                eng.tensor_copy(wxT[:, 2 * n:2 * n + 2, :], ps_x[n][:, :, :]).then_inc(kept, 1)
            eng.tensor_scalar(temp[:], temp[:], 0.1, 5.0, ALU.max, ALU.min).then_inc(chain, 1)
            eng.wait_ge(chain, 1)
            eng.reciprocal(temp[:], temp[:]).then_inc(chain, 1)
            eng.wait_ge(chain, 2)
            for m in range(2):
                eng.wait_ge(comp_mm, m + 1)
                eng.tensor_tensor(k.w_logit[:, m, :].rearrange("p (h g) -> p h g", g=G), ps_c[m][:, :, :],
                                  temp[:].unsqueeze(2).to_broadcast([128, 8, G]), ALU.mult)
            eng.wait_ge(comp_mm, 3)
            eng.tensor_tensor(row[:, :, :], ps_b[:, :, :], bs[:, :, :], ALU.add).then_inc(chain, 1)
            eng.wait_ge(chain, 3)
            eng.tensor_tensor(row[:, :, :], row[:, :, :], temp[0:1, :].unsqueeze(2).to_broadcast([1, 8, G]), ALU.mult)\
               .then_inc(chain, 1)
            eng.wait_ge(row_mm, 1)
            eng.tensor_copy(k.b_logit[:], ps_r[:, :])

        @block.tensor
        def _(eng):
            eng.wait_ge(w_in, 16 * 9)
            eng.wait_ge(ones_ready, 1)
            for m in range(2):
                for o in range(2):
                    mm = eng.transpose(ps_g[:, m, o * 128:(o + 1) * 128], wg[:, o, m * 128:(m + 1) * 128], k.ident[:, :])
            mm.then_inc(turned, 1)
            for c in range(4):
                for m in range(2):
                    mm = eng.transpose(ps_x[c // 2][:, c % 2, m * 128:(m + 1) * 128], wx[:, m, c * 128:(c + 1) * 128],
                                       k.ident[:, :])
                if c % 2:
                    mm.then_inc(turned, 1)
            eng.wait_ge(kept, 2)
            for m in range(2):
                for c in range(4):
                    mm = eng.matmul(ps_c[m][:, 2 * c:2 * c + 2, :], wxT[:, c, m * 128:(m + 1) * 128], pair[:],
                                    start=True, stop=True)
                mm.then_inc(comp_mm, 1)
            for c in range(4):
                mm = eng.matmul(ps_b[:, 2 * c:2 * c + 2, :], bx[:, c:c + 1], pair[:], start=True, stop=True)
            mm.then_inc(comp_mm, 1)
            eng.wait_ge(chain, 4)
            eng.matmul(ps_r[:, :], ones[:], row[:, :, :], start=True, stop=True).then_inc(row_mm, 1)


def slice_weights(nc, k):
    TE = 2
    NP = k.NT // TE
    G = 64
    with ExitStack() as ctx:
        sb, pb, sem = allocators(nc, ctx, "slices")
        x3 = sb("x3", [P, 2, TE, D])
        y2 = sb("y2", [P, 2, TE, D])
        sc = sb("sums_now", [P, TE, D])
        sT = sb("sums_T", [128, TE, 2, P])
        xn = sb("xn", [P, 2, TE, D + 1])
        xT = sb("xn_T", [128, TE, 2, P])
        sw = sb("sw", [P, 2, TE, 2 * D])
        peak, total = (sb(n, [P, TE, 8]) for n in ("peak", "total"))
        st = sb("stats", [P, TE, 6])
        mv = sb("mean_var", [P, 2, TE, 2])
        ve = sb("var_eps", [P, TE])
        rs = sb("rstds", [P, 2, TE])
        neg_half = sb("neg_half", [P, TE])
        ones = sb("ones", [1, P])
        zeros = sb("zeros", [1, D + 1])
        ps_T = pb("ps_T", [128, TE, 2, P])
        ps_M = pb("ps_M", [P, TE, D])
        ps_L = [pb(f"ps_L{j}", [P, 2 * D]) for j in range(TE)]
        ps_acc = [pb(f"ps_acc{c}", [128, D + 1]) for c in range(4)]
        x_in, x_out, w_out = ([sem(f"{name}{n}") for n in range(2)] for name in ("x_in", "x_out", "w_out"))
        names = ("consts", "power_ready", "s_copied", "Ts_done", "Ts_kept", "g_done", "m_ready", "x3_ready",
                 "st_done", "mv_ready", "rs_steps", "rs_ready", "xn_ready", "Tx_done", "Tx_kept", "l_done", "l_kept",
                 "chain", "l_less", "e_done", "sw_ready", "acc_done")
        S = Shared()
        (S.consts, S.power_ready, S.s_copied, S.Ts_done, S.Ts_kept, S.g_done, S.m_ready, S.x3_ready, S.st_done,
         S.mv_ready, S.rs_steps, S.rs_ready, S.xn_ready, S.Tx_done, S.Tx_kept, S.l_done, S.l_kept, S.chain, S.l_less,
         S.e_done, S.sw_ready, S.acc_done) = (sem(n) for n in names)
        block = ctx.enter_context(nc.Block())

        def pipeline(eng, run):
            run(0, 0, 0, weigh=False, sum_=False)
            run(1, 1, 0, sum_=False)
            run(2, 0, 1)
            run(3, 1, 1)
            with eng.Fori(2, NP // 2) as m:
                run(m * 2, 0, m)
                run(m * 2 + 1, 1, m)
            run(NP, 0, NP // 2, gcn=False)
            run(NP + 1, 1, NP // 2, gcn=False, weigh=False)

        def after(eng, sem_, count):
            if not isinstance(count, int) or count > 0:
                eng.wait_ge(sem_, count)

        def rows_of(p):
            return bass.ds(p * (TE * P), TE * P)

        def tiled(ap):
            return ap.rearrange("(t p) d -> p t d", p=P)

        @block.sync
        def _(eng):
            def load(p, n, turn):
                if not isinstance(p, int) or p > 1:
                    eng.wait_ge(S.xn_ready, (p - 1) * TE)
                    eng.nop(nofuse=True)
                    eng.wait_ge(x_out[n], turn * 16)
                    eng.nop(nofuse=True)
                eng.dma_start(x3[:, n, :, :], tiled(k.x2[rows_of(p), :])).then_inc(x_in[n], 16)
                eng.dma_start(y2[:, n, :, :], tiled(k.mixed[rows_of(p), :])).then_inc(x_in[n], 16)

            def run(i, n, turn, gcn=True, weigh=True, sum_=True):
                if gcn:
                    eng.wait_ge(S.x3_ready, i + 1)
                    eng.nop(nofuse=True)
                    eng.dma_start(tiled(k.x3[rows_of(i), :]), x3[:, n, :, :]).then_inc(x_out[n], 16)
                    if not isinstance(i, int):
                        load(i + 1, 1 - n, turn + n)
                    elif i + 1 < NP:
                        load(i + 1, 1 - n, (i + 1) // 2)
                if weigh:
                    eng.wait_ge(S.sw_ready, i * TE)
                    eng.nop(nofuse=True)
                    eng.dma_start(tiled(k.sw[rows_of(i - 1), :]), sw[:, 1 - n, :, :]).then_inc(w_out[1 - n], 16)

            load(0, 0, 0)
            run(0, 0, 0, weigh=False)
            run(1, 1, 0)
            with eng.Fori(1, NP // 2 - 1) as m:
                run(m * 2, 0, m)
                run(m * 2 + 1, 1, m)
            run(NP - 2, 0, NP // 2 - 1)
            run(NP - 1, 1, NP // 2 - 1)
            run(NP, 0, NP // 2, gcn=False)
            for n in range(2):
                eng.wait_ge(x_out[n], 16 * (NP // 2))
                eng.nop(nofuse=True)
                eng.wait_ge(w_out[n], 16 * (NP // 2))
                eng.nop(nofuse=True)

        @block.gpsimd
        def _(eng):
            eng.memset(neg_half[:], -0.5).then_inc(S.power_ready, 1)
            eng.memset(ones[:], 1.0).then_inc(S.consts, 1)
            eng.memset(zeros[:], 0.0).then_inc(S.consts, 1)
            eng.memset(xn[:, :, :, D:D + 1], 1.0).then_inc(S.consts, 1)
            eng.wait_ge(S.power_ready, 1)

            def run(i, n, turn, gcn=True, weigh=True, sum_=True):
                if gcn:
                    eng.wait_ge(S.mv_ready, i + 1)
                    eng.nop(nofuse=True)
                    eng.tensor_scalar(ve[:], mv[:, n, :, 1], LN_EPS, None, ALU.add).then_inc(S.rs_steps, 1)
                    eng.wait_ge(S.rs_steps, i + 1)
                    after(eng, S.xn_ready, (i - 1) * TE)
                    eng.nop(nofuse=True)
                    eng.tensor_tensor(rs[:, n, :], ve[:], neg_half[:], ALU.pow).then_inc(S.rs_ready, 1)

            pipeline(eng, run)

        @block.vector
        def _(eng):
            def heads(ap):
                return ap.rearrange("p (h g) -> p h g", g=G)

            def spread(ap):
                return ap.unsqueeze(2).to_broadcast([P, 8, G])

            def run(i, n, turn, gcn=True, weigh=True, sum_=True):
                p, b = i - 1, 1 - n
                if weigh:
                    eng.wait_ge(S.rs_ready, p + 1)
                    for j in range(TE):
                        after(eng, S.acc_done, (p - 2) * TE + j + 1)
                        eng.tensor_scalar(xn[:, b, j, 0:D], x3[:, b, j, :], mv[:, b, j, 0:1], rs[:, b, j:j + 1],
                                          ALU.subtract, ALU.mult).then_inc(S.xn_ready, 1)
                if gcn:
                    eng.wait_ge(x_in[n], turn * 32 + 32)
                    eng.tensor_tensor(y2[:, n, :, :], y2[:, n, :, :], x3[:, n, :, :], ALU.add).then_inc(S.m_ready, 1)
                    eng.wait_ge(S.g_done, i + 1)
                    eng.wait_ge(S.m_ready, i + 1)
                    eng.scalar_tensor_tensor(out=x3[:, n, :, :], in0=ps_M[:, :, :], scalar=0.0, in1=y2[:, n, :, :],
                                             op0=ALU.max, op1=ALU.add).then_inc(S.x3_ready, 1)
                    eng.wait_ge(S.x3_ready, i + 1)
                    after(eng, S.mv_ready, i)
                    for j in range(TE):
                        eng.bn_stats(st[:, j, :], x3[:, n, j, :]).then_inc(S.st_done, 1)
                    eng.wait_ge(S.st_done, i * TE + TE)
                    after(eng, S.xn_ready, (i - 1) * TE)
                    eng.nop(nofuse=True)
                    for j in range(TE):
                        ins = eng.bn_aggr(mv[:, n, j, :], st[:, j, :])
                    ins.then_inc(S.mv_ready, 1)
                if weigh:
                    for j in range(TE):
                        eng.wait_ge(S.l_done, p * TE + j + 1)
                        after(eng, S.acc_done, (p - 2) * TE + j + 1)
                        if not isinstance(p, int) or p > 1:
                            eng.wait_ge(w_out[b], (turn - 1 + n) * 16)
                        eng.tensor_tensor(sw[:, b, j, :], ps_L[j][:, :], k.b_logit[:], ALU.add).then_inc(S.l_kept, 1)
                    for j in range(TE):
                        eng.wait_ge(S.l_kept, p * TE + j + 1)
                        eng.tensor_reduce(peak[:, j, :], heads(sw[:, b, j, :]), AX.X, ALU.max).then_inc(S.chain, 1)
                    for j in range(TE):
                        eng.wait_ge(S.chain, p * 6 + j + 1)
                        eng.tensor_tensor(heads(sw[:, b, j, :]), heads(sw[:, b, j, :]), spread(peak[:, j, :]),
                                          ALU.subtract).then_inc(S.l_less, 1)
                    for j in range(TE):
                        eng.wait_ge(S.e_done, p * TE + j + 1)
                        eng.tensor_reduce(total[:, j, :], heads(sw[:, b, j, :]), AX.X, ALU.add).then_inc(S.chain, 1)
                    for j in range(TE):
                        eng.wait_ge(S.chain, p * 6 + j + 3)
                        eng.reciprocal(total[:, j, :], total[:, j, :]).then_inc(S.chain, 1)
                    for j in range(TE):
                        eng.wait_ge(S.chain, p * 6 + j + 5)
                        eng.tensor_tensor(heads(sw[:, b, j, :]), heads(sw[:, b, j, :]), spread(total[:, j, :]),
                                          ALU.mult).then_inc(S.sw_ready, 1)

            pipeline(eng, run)
            eng.wait_ge(S.acc_done, k.NT)
            for c in range(4):
                eng.tensor_copy(k.slice_acc[:, c, :], ps_acc[c][:, :])

        @block.scalar
        def _(eng):
            def copy_sums(p):
                after(eng, S.Ts_done, p)
                eng.copy(sc[:, :, :], k.sums[:, bass.ds(p * TE, TE), :]).then_inc(S.s_copied, 1)

            def run(i, n, turn, gcn=True, weigh=True, sum_=True):
                p, b = i - 1, 1 - n
                if gcn:
                    copy_sums(i)
                    eng.wait_ge(S.Ts_done, i + 1)
                    after(eng, S.g_done, i)
                    eng.copy(sT[:, :, :, :], ps_T[:, :, :, :]).then_inc(S.Ts_kept, 1)
                if weigh:
                    eng.wait_ge(S.Tx_done, p + 1)
                    after(eng, S.l_done, p * TE)
                    eng.copy(xT[:, :, :, :], ps_T[:, :, :, :]).then_inc(S.Tx_kept, 1)
                    for j in range(TE):
                        eng.wait_ge(S.l_less, p * TE + j + 1)
                        eng.activation(sw[:, b, j, :], sw[:, b, j, :], ACT.Exp).then_inc(S.e_done, 1)

            pipeline(eng, run)

        @block.tensor
        def _(eng):
            eng.wait_ge(S.consts, 3)
            for c in range(4):
                eng.matmul(ps_acc[c][:, :], zeros[:, 0:128], zeros[:, :], start=True, stop=False, skip_group_check=True)

            def turn_(src):
                for j in range(TE):
                    for c in range(2):
                        mm = eng.transpose(ps_T[:, j, c, :], src[:, j, c * H2:(c + 1) * H2], k.ident[0:P, 0:P])
                return mm

            def run(i, n, turn, gcn=True, weigh=True, sum_=True):
                p, b = i - 1, 1 - n
                if gcn:
                    eng.wait_ge(S.s_copied, i + 1)
                    after(eng, S.Tx_kept, i - 1)
                    turn_(sc).then_inc(S.Ts_done, 1)
                    eng.wait_ge(S.Ts_kept, i + 1)
                    after(eng, S.x3_ready, i)
                    eng.matmul(ps_M[:, :, :], ones[:], k.b_gnn2[:, :, :], start=True, stop=False, skip_group_check=True)
                    for j in range(TE):
                        for c in range(2):
                            mm = eng.matmul(ps_M[:, j, :], sT[:, j, c, :], k.w_gnn[:, c, :], start=False, stop=False,
                                            skip_group_check=True)
                    mm.then_inc(S.g_done, 1)
                if weigh:
                    eng.wait_ge(S.xn_ready, p * TE + TE)
                    if not gcn:
                        eng.wait_ge(S.Tx_kept, p)
                    turn_(xn[:, b, :, :]).then_inc(S.Tx_done, 1)
                if sum_:
                    for j in range(TE):
                        eng.wait_ge(S.sw_ready, (i - 2) * TE + j + 1)
                        for c in range(4):
                            mm = eng.matmul(ps_acc[c][:, :], sw[:, n, j, c * 128:(c + 1) * 128], xn[:, n, j, :],
                                            start=False, stop=False, skip_group_check=True)
                        mm.then_inc(S.acc_done, 1)
                if weigh:
                    eng.wait_ge(S.Tx_kept, p + 1)
                    for j in range(TE):
                        after(eng, S.l_kept, (p - 1) * TE + j + 1)
                        for c in range(2):
                            mm = eng.matmul(ps_L[j][:, :], xT[:, j, c, :], k.w_logit[:, c, :], start=(c == 0), stop=(c == 1))
                        mm.then_inc(S.l_done, 1)

            pipeline(eng, run)


def slice_attention(nc, k):
    G = 64
    with ExitStack() as ctx:
        sb, pb, sem = allocators(nc, ctx, "sattn")
        wfx = sb("wfx", [128, 2, 2 * D])
        bfx = sb("bfx", [1, 2 * D])
        wo = sb("wo", [128, 4, D])
        pairs = [sb(f"pair_{n}", [128, 128]) for n in "qkv"]
        mask = sb("mask", [128, 2, G])
        accT = sb("acc_T", [128, 2, 4 * 128])
        norm = sb("norm_row", [1, 4 * 128])
        scale = sb("scale", [128, 4])
        tok, tokT, qT, kT, v, at, atT, oT = (sb(n, [128, 4, 128]) for n in
                                             ("tok", "tok_T", "q_T", "k_T", "v", "attn", "attn_T", "out_T"))
        peak, total = (sb(n, [128, 4]) for n in ("peak", "total"))
        ps = [pb(f"ps{n}", [128, 4, 128]) for n in range(3)]
        ps_n = pb("ps_n", [1, 4 * 128])
        ps_o = [pb(f"ps_o{n}", [128, 2, D]) for n in range(2)]
        w_in, cleared, masked, T_done, n_done, scale_steps, kept, mm_done = (
            sem(n) for n in ("w_in", "cleared", "masked", "T_done", "n_done", "scale_steps", "kept", "mm_done"))
        exp_ready, exp_done = sem("exp_ready"), sem("exp_done")
        chain = sem("chain")
        block = ctx.enter_context(nc.Block())

        @block.sync
        def _(eng):
            eng.dma_start(wfx[:, :, :], k.L1_ffn_W_fx.rearrange("(c p) n -> p c n", c=2)).then_inc(w_in, 16)
            eng.dma_start(bfx[:], k.L1_ffn_b_fx.rearrange("(a n) -> a n", a=1)).then_inc(w_in, 16)
            eng.dma_start(wo[:, :, :], k.L1_ffn_W_out.rearrange("(c p) n -> p c n", c=4)).then_inc(w_in, 16)
            eng.wait_ge(cleared, 3)
            eng.nop(nofuse=True)
            for tile, w in zip(pairs, (k.L1_ffn_W_q, k.L1_ffn_W_k, k.L1_ffn_W_v)):
                eng.dma_start(tile[0:G, 0:G], w).then_inc(w_in, 16)
                eng.dma_start(tile[G:128, G:128], w).then_inc(w_in, 16)

        @block.gpsimd
        def _(eng):
            for tile in pairs:
                eng.memset(tile[:], 0.0).then_inc(cleared, 1)
            eng.memset(mask[:, :, :], 0.0).then_inc(masked, 1)
            eng.wait_ge(masked, 1)
            eng.memset(mask[0:G, 0, :], 1.0).then_inc(masked, 1)
            eng.memset(mask[G:128, 1, :], 1.0).then_inc(masked, 1)

        @block.tensor
        def _(eng):
            eng.wait_ge(w_in, 16 * 9)
            for m in range(2):
                for c in range(4):
                    mm = eng.transpose(ps[m][:, c, :], k.slice_acc[:, c, m * 128:(m + 1) * 128], k.ident[:, :])
                mm.then_inc(T_done, 1)
            for c in range(4):
                mm = eng.transpose(ps_n[:, c * 128:(c + 1) * 128], k.slice_acc[:, c, D:D + 1], k.ident[:, :])
            mm.then_inc(T_done, 1)
            eng.wait_ge(kept, 3)
            for c in range(4):
                cols = slice(c * 128, (c + 1) * 128)
                for m in range(2):
                    eng.matmul(ps[2][:, c, :], accT[:, m, cols], wfx[:, m, cols], start=(m == 0), stop=False,
                               skip_group_check=True)
                mm = eng.matmul(ps[2][:, c, :], norm[:, cols], bfx[:, cols], start=False, stop=True,
                                skip_group_check=True)
            mm.then_inc(mm_done, 1)
            eng.wait_ge(kept, 4)
            for c in range(4):
                mm = eng.transpose(ps[0][:, c, :], tok[:, c, :], k.ident[:, :])
            mm.then_inc(mm_done, 1)
            eng.wait_ge(kept, 5)
            for n, out in ((0, ps[1]), (1, ps[2])):
                for c in range(4):
                    mm = eng.matmul(out[:, c, :], pairs[n][:], tokT[:, c, :], start=True, stop=True)
                mm.then_inc(mm_done, 1)
            for c in range(4):
                mm = eng.matmul(ps[0][:, c, :], tokT[:, c, :], pairs[2][:], start=True, stop=True)
            mm.then_inc(mm_done, 1)
            eng.wait_ge(kept, 7)
            for c in range(4):
                mm = eng.matmul(ps[1][:, c, :], qT[:, c, :], kT[:, c, :], start=True, stop=True)
            mm.then_inc(mm_done, 1)
            eng.wait_ge(kept, 9)
            for c in range(4):
                mm = eng.transpose(ps[2][:, c, :], at[:, c, :], k.ident[:, :])
            mm.then_inc(mm_done, 1)
            eng.wait_ge(kept, 10)
            for c in range(4):
                mm = eng.matmul(ps[0][:, c, :], v[:, c, :], atT[:, c, :], start=True, stop=True)
            mm.then_inc(mm_done, 1)
            eng.wait_ge(kept, 11)
            for c in range(4):
                mm = eng.matmul(ps_o[c // 2][:, c % 2, :], oT[:, c, :], wo[:, c, :], start=True, stop=True)
            mm.then_inc(mm_done, 1)

        @block.scalar
        def _(eng):
            eng.wait_ge(exp_ready, 1)
            eng.activation(at[:, :, :], at[:, :, :], ACT.Exp, scale=float(G) ** -0.5).then_inc(exp_done, 1)

        @block.vector
        def _(eng):
            same_head = mask[:, :, :].rearrange("p h g -> p (h g)").unsqueeze(1).to_broadcast([128, 4, 128])
            eng.tensor_scalar(scale[:], k.slice_acc[:, :, D], 1e-5, None, ALU.add).then_inc(scale_steps, 1)
            eng.wait_ge(scale_steps, 1)
            eng.reciprocal(scale[:], scale[:]).then_inc(scale_steps, 1)
            eng.wait_ge(scale_steps, 2)
            for m in range(2):
                eng.wait_ge(T_done, m + 1)
                eng.tensor_copy(accT[:, m, :].rearrange("p (c s) -> p c s", c=4), ps[m][:, :, :]).then_inc(kept, 1)
            eng.wait_ge(T_done, 3)
            eng.tensor_copy(norm[:], ps_n[:, :]).then_inc(kept, 1)
            eng.wait_ge(masked, 3)
            eng.wait_ge(mm_done, 1)
            eng.tensor_tensor(tok[:, :, :], ps[2][:, :, :], same_head, ALU.mult).then_inc(chain, 1)
            eng.wait_ge(chain, 1)
            eng.tensor_tensor(tok[:, :, :], tok[:, :, :], scale[:].unsqueeze(2).to_broadcast([128, 4, 128]), ALU.mult)\
               .then_inc(kept, 1)
            eng.wait_ge(mm_done, 2)
            eng.tensor_copy(tokT[:, :, :], ps[0][:, :, :]).then_inc(kept, 1)
            for n, out, bank in ((3, qT, 1), (4, kT, 2), (5, v, 0)):
                eng.wait_ge(mm_done, n)
                eng.tensor_copy(out[:, :, :], ps[bank][:, :, :]).then_inc(kept, 1)
            eng.wait_ge(mm_done, 6)
            own = [slice(0, G), slice(G, 128)]
            for h in range(2):
                eng.tensor_reduce(peak[own[h], :], ps[1][own[h], :, own[h]], AX.X, ALU.max).then_inc(chain, 1)
            eng.wait_ge(chain, 3)
            eng.tensor_tensor(at[:, :, :], ps[1][:, :, :], peak[:].unsqueeze(2).to_broadcast([128, 4, 128]),
                              ALU.subtract).then_inc(chain, 1)
            eng.wait_ge(chain, 4)
            eng.tensor_scalar(at[:, :, :], at[:, :, :], 0.0, None, ALU.min).then_inc(exp_ready, 1)
            eng.wait_ge(exp_done, 1)
            eng.tensor_tensor(at[:, :, :], at[:, :, :], same_head, ALU.mult).then_inc(chain, 1)
            eng.wait_ge(chain, 5)
            eng.tensor_reduce(total[:], at[:, :, :], AX.X, ALU.add).then_inc(chain, 1)
            eng.wait_ge(chain, 6)
            eng.reciprocal(total[:], total[:]).then_inc(chain, 1)
            eng.wait_ge(chain, 7)
            eng.tensor_tensor(at[:, :, :], at[:, :, :], total[:].unsqueeze(2).to_broadcast([128, 4, 128]), ALU.mult)\
               .then_inc(kept, 1)
            eng.wait_ge(mm_done, 7)
            eng.tensor_copy(atT[:, :, :], ps[2][:, :, :]).then_inc(kept, 1)
            eng.wait_ge(mm_done, 8)
            eng.tensor_copy(oT[:, :, :], ps[0][:, :, :]).then_inc(kept, 1)
            eng.wait_ge(mm_done, 9)
            for n in range(2):
                eng.tensor_copy(k.slice_out[:, 2 * n:2 * n + 2, :], ps_o[n][:, :, :])


def write_out(nc, k):
    TE = 2
    NP = k.NT // TE
    with ExitStack() as ctx:
        sb, pb, sem = allocators(nc, ctx, "out")
        bo = sb("b_out", [1, TE, D])
        ones = sb("ones", [1, P])
        x3 = sb("x3", [P, 4, TE, D])
        sw = sb("sw", [P, 4, TE, 2 * D])
        swT = sb("sw_T", [128, 2, TE, 4, P])
        res = sb("res", [P, 2, TE, D])
        ps_T = [[pb(f"ps_T{n}{j}", [128, 4, P]) for j in range(TE)] for n in range(2)]
        ps_o = [pb(f"ps_o{n}", [P, TE, D]) for n in range(2)]
        in_ = [sem(f"in{n}") for n in range(4)]
        out_ = [sem(f"out{n}") for n in range(2)]
        b_in, ones_ready, turned, done, added = (sem(n) for n in ("b_in", "ones_ready", "turned", "done", "added"))
        kept = [sem(f"kept{j}") for j in range(TE)]
        block = ctx.enter_context(nc.Block())

        def pairs(eng, run):
            for i in range(6):
                run(i, i % 4, i // 4)
            with eng.Fori(1, (NP - 2) // 4) as m:
                for q in range(4):
                    run(m * 4 + (q + 2), (q + 2) % 4, m + (q + 2) // 4)

        def after(eng, sem_, count):
            if not isinstance(count, int) or count > 0:
                eng.wait_ge(sem_, count)

        def rows_of(p):
            return bass.ds(p * (TE * P), TE * P)

        def tiled(ap):
            return ap.rearrange("(t p) d -> p t d", p=P)

        @block.sync
        def _(eng):
            for j in range(TE):
                eng.dma_start(bo[:, j, :], k.L1_ffn_b_out.rearrange("(a n) -> a n", a=1)).then_inc(b_in, 16)

            def run(i, n, turn):
                after(eng, turned, (i - 3) * TE)
                eng.nop(nofuse=True)
                after(eng, added, i - 3)
                eng.nop(nofuse=True)
                eng.dma_start(x3[:, n, :, :], tiled(k.x3[rows_of(i), :])).then_inc(in_[n], 16)
                eng.dma_start(sw[:, n, :, :], tiled(k.sw[rows_of(i), :])).then_inc(in_[n], 16)

            pairs(eng, run)

        @block.gpsimd
        def _(eng):
            eng.memset(ones[:], 1.0).then_inc(ones_ready, 1)

            def run(i, n, turn):
                eng.wait_ge(added, i + 1)
                eng.dma_start(tiled(k.out[rows_of(i), :]), res[:, n % 2, :, :]).then_inc(out_[n % 2], 16)

            pairs(eng, run)
            for n in range(2):
                eng.wait_ge(out_[n], 16 * (NP // 2))

        def keep(eng, copy, i, n, j):
            eng.wait_ge(turned, i * TE + j + 1)
            after(eng, done, i - 1)
            copy(swT[:, n % 2, j, :, :], ps_T[n % 2][j][:, :, :]).then_inc(kept[j], 1)

        @block.scalar
        def _(eng):
            pairs(eng, lambda i, n, turn: keep(eng, eng.copy, i, n, 0))

        @block.vector
        def _(eng):
            def run(i, n, turn):
                keep(eng, eng.tensor_copy, i, n, 1)
                eng.wait_ge(done, i + 1)
                after(eng, out_[n % 2], (turn * 2 + n // 2) * 16)
                eng.tensor_tensor(res[:, n % 2, :, :], ps_o[n % 2][:, :, :], x3[:, n, :, :], ALU.add).then_inc(added, 1)

            pairs(eng, run)

        @block.tensor
        def _(eng):
            eng.wait_ge(b_in, 32)
            eng.wait_ge(ones_ready, 1)

            def turn_(i, n, turn):
                eng.wait_ge(in_[n], turn * 32 + 32)
                for j in range(TE):
                    after(eng, kept[j], i - 1)
                    for c in range(4):
                        mm = eng.transpose(ps_T[n % 2][j][:, c, :], sw[:, n, j, c * 128:(c + 1) * 128], k.ident[0:P, 0:P])
                    mm.then_inc(turned, 1)

            def product(i, n):
                after(eng, added, i - 1)
                eng.matmul(ps_o[n][:, :, :], ones[:], bo[:, :, :], start=True, stop=False, skip_group_check=True)
                for j in range(TE):
                    eng.wait_ge(kept[j], i + 1)
                    for c in range(4):
                        mm = eng.matmul(ps_o[n][:, j, :], swT[:, n, j, c, :], k.slice_out[:, c, :], start=False,
                                        stop=False, skip_group_check=True)
                mm.then_inc(done, 1)

            def run(i, n, turn):
                turn_(i, n, turn)
                if not isinstance(i, int) or i > 0:
                    product(i - 1, 1 - n % 2)

            pairs(eng, run)
            product(NP - 1, 1)


def whole(nc, **t):
    k = Shared()
    k.out = t["out"]
    (k.x, k.src, k.dst, k.edge_weight, k.L0_gnn_W, k.L0_gnn_b, k.L0_gnn_gamma, k.L0_gnn_beta, k.L0_mix_Wqkv,
     k.L0_mix_Wout, k.L0_mix_gamma, k.L0_ffn_router_w, k.L0_ffn_w1, k.L0_ffn_b1, k.L0_ffn_w2, k.L0_ffn_b2, k.L1_gnn_W,
     k.L1_gnn_bias, k.L1_mix_Wq, k.L1_mix_bq, k.L1_mix_Wk, k.L1_mix_bk, k.L1_mix_Wv, k.L1_mix_bv, k.L1_mix_Wo,
     k.L1_mix_bo, k.L1_mix_W1, k.L1_mix_b1, k.L1_mix_W2, k.L1_mix_b2, k.L1_mix_ln1_g, k.L1_mix_ln1_b, k.L1_mix_ln2_g,
     k.L1_mix_ln2_b, k.L1_ffn_W_fx, k.L1_ffn_b_fx, k.L1_ffn_W_x, k.L1_ffn_b_x, k.L1_ffn_W_slice, k.L1_ffn_b_slice,
     k.L1_ffn_W_q, k.L1_ffn_W_k, k.L1_ffn_W_v, k.L1_ffn_W_out, k.L1_ffn_b_out, k.L1_ffn_temperature) = (t[n] for n in _INS)
    N, E = t["x"].shape[0], t["src"].shape[0]
    k.N, k.NT, k.NSUP, k.ROWS = N, N // P, N // (P * TS), E // P
    k.NS = k.NSUP * STEPS
    k.CR = k.ROWS // k.NT
    k.RPS = k.ROWS // k.NSUP
    assert N == k.NSUP * P * TS and E == k.ROWS * P and k.ROWS + k.NT - 1 <= k.NS and k.ROWS % k.NT == 0
    k.dst_rows, k.src_rows, k.w_rows = (t[n].rearrange("(r e) -> r e", e=P) for n in ("dst", "src", "edge_weight"))
    with ExitStack() as ctx:
        sb, pb, sem = allocators(nc, ctx, "all")
        k.ident = sb("ident", [128, 128])
        k.lane = sb("lane", [128, 128])
        k.mean, k.rstd, k.dinv, k.scale0 = (sb(n, [P, k.NT]) for n in ("mean", "rstd", "dinv", "scale0"))
        k.key_max = sb("key_max", [P, D])
        k.context = sb("context", [128, 2, D + 1])
        k.bucket_start = sb("bucket_start", [k.NT + 1, 1])
        k.table0, k.table1 = (nc.dram_tensor(n, [k.N, D], F32, kind="Internal").ap() for n in ("table0", "table1"))
        k.mixed = nc.dram_tensor("mixed", [k.N, D], F32, kind="Internal").ap()
        k.x3 = nc.dram_tensor("x3", [k.N, D], F32, kind="Internal").ap()
        k.sw = nc.dram_tensor("slice_weights", [k.N, 2 * D], F32, kind="Internal").ap()
        k.x2 = nc.dram_tensor("x2", [k.N, D], F32, kind="Internal").ap()
        k.rec_d = nc.dram_tensor("rec_d", [P, k.ROWS, 3], I32, kind="Internal").ap()
        k.pos_d = nc.dram_tensor("pos_d", [P, k.ROWS], I32, kind="Internal").ap()
        k.sorted_recs = nc.dram_tensor("sorted_recs", [E, 3], I32, kind="Internal").ap()
        k.sorted_rows = k.sorted_recs.rearrange("(r e) f -> r (e f)", e=P)
        k.sums = sb("sums", [P, k.NT + 1, D])
        k.composed = sb("composed", [128, 2, D])
        k.key_sum_of = sb("key_sum_of", [128, 2, 128])
        with ExitStack() as scope:
            sb, pb, sem = allocators(nc, scope, "steps0")
            step_lists(k, sb)
            k.src_tile = sb("src_tile", [P, k.ROWS + 4], BF16)
            k.rank_start = sb("rank_start", [P, 4, 100])
            with ExitStack() as first:
                sb, pb, sem = allocators(nc, first, "first")
                k.hist = sb("hist", [10, 4, 10])
                k.digit_hi = sb("digit_hi", [P, k.ROWS], BF16)
                k.digit_lo = sb("digit_lo", [P, k.ROWS], BF16)
                records(nc, k)
                plan(nc, k, 0)
                with nc.sbuf_tensor("deg_step", [128, k.NS], F32) as k.deg_step:
                    degrees_and_key_max(nc, k)
                    degree_scales(nc, k)
            scale_rows(nc, k)
            sum_layer0(nc, k)
        compose(nc, k, 0)
        finish_layer0(nc, k)
        compose(nc, k, 1)
        with ExitStack() as scope:
            sb, pb, sem = allocators(nc, scope, "steps1")
            step_lists(k, sb)
            plan(nc, k, 1)
            sum_layer1(nc, k)
        with ExitStack() as scope:
            sb, pb, sem = allocators(nc, scope, "last")
            k.w_gnn = sb("w_gnn", [128, 2, D])
            k.w_logit = sb("w_logit", [128, 2, 2 * D])
            k.b_logit = sb("b_logit", [P, 2 * D])
            k.b_gnn2 = sb("b_gnn2", [1, 2, D])
            k.slice_acc = sb("slice_acc", [128, 4, D + 1])
            k.slice_out = sb("slice_out", [128, 4, D])
            prepare_slices(nc, k)
            slice_weights(nc, k)
            slice_attention(nc, k)
            write_out(nc, k)


def step_lists(k, sb):
    k.src_p = sb("src_p", [P, k.NS], I32)
    k.dloc_p = sb("dloc_p", [P, k.NS + GRP])
    k.w_p = sb("w_p", [P, k.NS + GRP])
    k.tile_col = sb("tile_col", [1, k.NS], I32)
    k.tile_of = sb("tile_of", [SG, k.NS // SG])


_INS = ['x', 'src', 'dst', 'edge_weight', 'L0_gnn_W', 'L0_gnn_b', 'L0_gnn_gamma', 'L0_gnn_beta', 'L0_mix_Wqkv',
        'L0_mix_Wout', 'L0_mix_gamma', 'L0_ffn_router_w', 'L0_ffn_w1', 'L0_ffn_b1', 'L0_ffn_w2', 'L0_ffn_b2',
        'L1_gnn_W', 'L1_gnn_bias', 'L1_mix_Wq', 'L1_mix_bq', 'L1_mix_Wk', 'L1_mix_bk', 'L1_mix_Wv', 'L1_mix_bv',
        'L1_mix_Wo', 'L1_mix_bo', 'L1_mix_W1', 'L1_mix_b1', 'L1_mix_W2', 'L1_mix_b2', 'L1_mix_ln1_g',
        'L1_mix_ln1_b', 'L1_mix_ln2_g', 'L1_mix_ln2_b', 'L1_ffn_W_fx', 'L1_ffn_b_fx', 'L1_ffn_W_x', 'L1_ffn_b_x',
        'L1_ffn_W_slice', 'L1_ffn_b_slice', 'L1_ffn_W_q', 'L1_ffn_W_k', 'L1_ffn_W_v', 'L1_ffn_W_out',
        'L1_ffn_b_out', 'L1_ffn_temperature']


def kernel(**inputs):
    import numpy as np
    import concourse.bacc as bacc
    from concourse import mybir as _mybir
    from concourse.bass_utils import run_bass_kernel_spmd

    nc = bacc.Bacc("TRN2", target_bir_lowering=False, num_devices=1)
    arrays, aps = {}, {}
    for name in _INS:
        a = np.ascontiguousarray(inputs[name])
        arrays[f"in_{name}"] = a
        aps[name] = nc.dram_tensor(f"in_{name}", a.shape, _mybir.dt.from_np(a.dtype), kind="ExternalInput").ap()
    out = nc.dram_tensor("out_x", inputs["x"].shape, _mybir.dt.float32, kind="ExternalOutput").ap()
    whole(nc, out=out, **aps)
    r = run_bass_kernel_spmd(nc, [arrays], core_ids=[0])
    return r.results[0]["out_x"]
```
